# Optimizing a Trainium2 kernel written in Bass

```python
import numpy as np
import jax
import jax.numpy as jnp

def _softmax(x, axis=-1):
    return jax.nn.softmax(x, axis=axis)

def _gelu(x):
    return jax.nn.gelu(x, approximate=True)

def _silu(x):
    return jax.nn.silu(x)

def _sigmoid(x):
    return jax.nn.sigmoid(x)

def _layernorm(x, axis=-1, eps=1e-05):
    m = jnp.mean(x, axis=axis, keepdims=True)
    v = jnp.var(x, axis=axis, keepdims=True)
    return (x - m) / jnp.sqrt(v + eps)

def _scatter_add(tgt, idx, src, axis=0):
    return tgt.at[idx].add(src)

def _segment_sum(src, seg, n):
    return jax.ops.segment_sum(src, seg, n)
kernel_name = 'mk_adj_resnorm_d2_adj_r2_e969e7'

def setup_inputs(seed: int=0):
    np.random.seed(seed)
    _w = jnp.asarray

    def _rec_inputs():
        import jax
        import jax.numpy as jnp
        _gk = jax.random.key(seed)
        x = -0.0002928 + 1 * jax.random.normal(jax.random.fold_in(_gk, 1), (8, 1024, 128), jnp.float32)
        _w = (1.0 + jnp.arange(1024, dtype=jnp.float32)) ** (-0.5)
        _w = _w / _w.mean()
        _pij = jnp.clip(0.00195312 * _w[:, None] * _w[None, :], 0.0, 1.0)
        _a = jax.random.uniform(jax.random.fold_in(_gk, 2), (8, 1024, 1024)) < _pij
        _af = _a.astype(jnp.float32)
        adj = _af
        return (x, adj)
    x, adj = _rec_inputs()

    def _L0_gnn_setup():
        import jax, jax.numpy as jnp
        import numpy as np
        H = 128
        EPS_RENORM = 1e-10
        EPS_LN = 1e-12
        key = jax.random.key(seed)
        ks = jax.random.split(key, 10)
        B, N = (8, 1024)
        hidden_state = jax.random.normal(ks[0], (B, N, H), dtype=jnp.float32)
        adjacency_matrix = jax.random.randint(ks[1], (B, N, N), 0, 2).astype(jnp.float32)

        def lin(kw, kb):
            W = jax.random.normal(kw, (H, H), dtype=jnp.float32) * (2.0 / (H + H)) ** 0.5
            bound = 1.0 / np.sqrt(H)
            b = jax.random.uniform(kb, (H,), minval=-bound, maxval=bound, dtype=jnp.float32)
            return (W, b)
        Wl, bl = lin(ks[2], ks[3])
        Ws, bs = lin(ks[4], ks[5])
        Wr, br = lin(ks[6], ks[7])
        ln_w = jnp.ones((H,), dtype=jnp.float32)
        ln_b = jnp.zeros((H,), dtype=jnp.float32)
        return {'hidden_state': hidden_state, 'adjacency_matrix': adjacency_matrix, 'Wl': Wl, 'bl': bl, 'Ws': Ws, 'bs': bs, 'Wr': Wr, 'br': br, 'ln_w': ln_w, 'ln_b': ln_b}
    _L0_gnn_all = _L0_gnn_setup()
    _L0_gnn_in = {k: v for k, v in _L0_gnn_all.items() if k in ('Wl', 'bl', 'Ws', 'bs', 'Wr', 'br', 'ln_w', 'ln_b')}
    del _L0_gnn_all

    def _L1_gnn_setup():
        import jax, jax.numpy as jnp
        import numpy as np
        B, N, C_IN, C_OUT = (8, 1024, 128, 128)
        key = jax.random.key(seed)
        k1, k2, k3 = jax.random.split(key, 3)
        x = jax.random.normal(k1, (B, N, C_IN), dtype=jnp.float32)
        adj = jax.random.uniform(k2, (B, N, N), dtype=jnp.float32)
        limit = float(np.sqrt(6.0 / (C_IN + C_OUT)))
        weight = jax.random.uniform(k3, (C_IN, C_OUT), minval=-limit, maxval=limit, dtype=jnp.float32)
        bias = jnp.zeros((C_OUT,), dtype=jnp.float32)
        return {'x': x, 'adj': adj, 'weight': weight, 'bias': bias}
    _L1_gnn_all = _L1_gnn_setup()
    _L1_gnn_in = {k: v for k, v in _L1_gnn_all.items() if k in ('weight', 'bias')}
    del _L1_gnn_all
    return {'x': x, 'adj': adj, 'L0_gnn_Wl': _L0_gnn_in['Wl'], 'L0_gnn_bl': _L0_gnn_in['bl'], 'L0_gnn_Ws': _L0_gnn_in['Ws'], 'L0_gnn_bs': _L0_gnn_in['bs'], 'L0_gnn_Wr': _L0_gnn_in['Wr'], 'L0_gnn_br': _L0_gnn_in['br'], 'L0_gnn_ln_w': _L0_gnn_in['ln_w'], 'L0_gnn_ln_b': _L0_gnn_in['ln_b'], 'L1_gnn_weight': _L1_gnn_in['weight'], 'L1_gnn_bias': _L1_gnn_in['bias']}

def reference(x, adj, L0_gnn_Wl, L0_gnn_bl, L0_gnn_Ws, L0_gnn_bs, L0_gnn_Wr, L0_gnn_br, L0_gnn_ln_w, L0_gnn_ln_b, L1_gnn_weight, L1_gnn_bias):
    import jax
    import jax.numpy as jnp

    def _L0_gnn_ref(hidden_state, adjacency_matrix, Wl, bl, Ws, bs, Wr, br, ln_w, ln_b):
        import jax, jax.numpy as jnp
        import numpy as np
        H = 128
        EPS_RENORM = 1e-10
        EPS_LN = 1e-12
        B, N, Hd = hidden_state.shape
        temper = Hd ** 0.5
        u = jnp.einsum('bnh,bmh->bnm', hidden_state, hidden_state) / temper
        scores = jax.nn.softmax(u, axis=-1)
        delta = scores * adjacency_matrix
        att = delta / (jnp.sum(delta, axis=2, keepdims=True) + EPS_RENORM)
        i = jnp.arange(N)[:, None]
        j = jnp.arange(N)[None, :]
        att_left = jnp.where(j > i, att, 0.0)
        att_self = jnp.where(j == i, att, 0.0)
        att_right = jnp.where(j < i, att, 0.0)
        h_left = hidden_state @ Wl.T + bl
        h_self = hidden_state @ Ws.T + bs
        h_right = hidden_state @ Wr.T + br
        ctx = jnp.einsum('bnm,bmh->bnh', att_left, h_left) + jnp.einsum('bnm,bmh->bnh', att_self, h_self) + jnp.einsum('bnm,bmh->bnh', att_right, h_right)
        mu = jnp.mean(ctx, axis=-1, keepdims=True)
        var = jnp.mean((ctx - mu) ** 2, axis=-1, keepdims=True)
        o = ln_w * ((ctx - mu) / jnp.sqrt(var + EPS_LN)) + ln_b
        return jax.nn.relu(o)

    def _L1_gnn_ref(x, adj, weight, bias):
        import jax, jax.numpy as jnp
        import numpy as np
        B, N, C_IN, C_OUT = (8, 1024, 128, 128)
        d_inv_sqrt = (jnp.sum(adj, axis=-1) + 1e-05) ** (-0.5)
        adj_norm = d_inv_sqrt[..., :, None] * adj * d_inv_sqrt[..., None, :]
        support = jnp.einsum('bni,io->bno', x, weight)
        return jnp.einsum('bnm,bmo->bno', adj_norm, support) + bias
    x = _layernorm(x + _L0_gnn_ref(x, adj, L0_gnn_Wl, L0_gnn_bl, L0_gnn_Ws, L0_gnn_bs, L0_gnn_Wr, L0_gnn_br, L0_gnn_ln_w, L0_gnn_ln_b), axis=-1)
    x = _layernorm(x + _L1_gnn_ref(x, adj, L1_gnn_weight, L1_gnn_bias), axis=-1)
    return x

_drawn_inputs = setup_inputs


def setup_inputs(seed=0):
    import zlib

    import numpy as np

    out = dict(_drawn_inputs(seed))
    spreads = {'L0_gnn_ln_w': (1.0, 0.2), 'L0_gnn_ln_b': (0.0, 0.1), 'L1_gnn_bias': (0.0, 0.1)}
    factors = {'L0_gnn_bl': 3.313, 'L0_gnn_bs': 8.0}
    for name, (base, spread) in spreads.items():
        noise = np.random.default_rng([zlib.crc32(name.encode()), seed]).standard_normal(out[name].shape)
        drawn = base * np.exp(spread * noise) if base else spread * noise
        out[name] = jnp.asarray(drawn.astype(out[name].dtype))
    for name, factor in factors.items():
        out[name] = (out[name] * factor).astype(out[name].dtype)
    return out
```

```python
from contextlib import ExitStack

import concourse.bass as bass
from concourse import mybir

F32 = mybir.dt.float32
F32R = mybir.dt.float32r
ALU = mybir.AluOpType
ACT = mybir.ActivationFunctionType
AX = mybir.AxisListType

P = 128
EPS_RENORM = 1e-10
EPS_CTX = 1e-12
EPS_LN = 1e-5
EPS_DEG = 1e-5


def wait(eng, sem, value):
    if isinstance(value, int) and value <= 0:
        return
    eng.wait_ge(sem, value)


def two_layer_graph_kernel(nc, x, adj, Wl, bl, Ws, bs, Wr, br, ln_w, ln_b, W1, b1, out):
    B, N, H = x.shape
    NB = N // P
    HB = NB // 2
    HALF = N // 2
    SCALE = float(H) ** -0.5
    assert H == P and NB == 8 and HALF == 512

    with ExitStack() as ctx:
        def sb(name, shape, dt=F32):
            return ctx.enter_context(nc.sbuf_tensor(name, shape, dt))

        def pb(name, shape):
            return ctx.enter_context(nc.psum_tensor(name, shape, F32))

        def sem(name):
            return ctx.enter_context(nc.semaphore(name))

        ident = sb("ident", [P, P])
        ones = sb("ones", [64, P], F32R)
        onesf = sb("onesf", [64, P])
        sides = sb("sides", [P, 2 * P])
        wraw = sb("wraw", [P, 3, H])
        wT_hi = sb("wT_hi", [P, 3 * H], F32R)
        wT_lo = sb("wT_lo", [P, 3 * H], F32R)
        brow = sb("brow", [64, 3 * H])
        brow_hi = sb("brow_hi", [64, 3 * H], F32R)
        bias2 = sb("bias2", [64, 3 * H], F32R)
        w1_sb = sb("w1_sb", [P, H])
        lnw_bc = sb("lnw_bc", [P, H])
        lnb_bc = sb("lnb_bc", [P, H])
        b1_bc = sb("b1_bc", [P, H])

        x_rows = sb("x_rows", [P, NB, H])
        x_res = sb("x_res", [P, NB, H])
        xT_hi = sb("xT_hi", [P, N], F32R)
        xT_lo = sb("xT_lo", [P, N], F32R)
        h_hi = sb("h_hi", [P, NB, 2 * H], F32R)
        h_lo = sb("h_lo", [P, NB, 2 * H], F32R)
        h_self = sb("h_self", [P, NB, H])
        a_rows = sb("a_rows", [P, NB, N])
        aT = sb("aT", [P, NB, N])
        e_rows = sb("e_rows", [P, 2, N])
        d_rows = sb("d_rows", [P, 2, N])
        dT_hi = sb("dT_hi", [P, NB, HALF + P], F32R)
        dT_lo = sb("dT_lo", [P, NB, HALF + P], F32R)
        ctxT = sb("ctxT", [P, HALF])
        yT = sb("yT", [P, 2, HALF])
        c_rows = sb("c_rows", [P, HB, H])
        x1 = sb("x1", [P, NB, H])
        x1p = sb("x1p", [P, NB, H])
        x1b = sb("x1b", [P, NB, H])
        fin = sb("fin", [P, 2, HB, H])
        fold = sb("fold", [P, HALF])
        fold2 = sb("fold2", [P, HALF // 2])
        fold3 = sb("fold3", [P, P])
        junk = sb("junk", [P, P])
        stats = sb("stats", [P, HB, 6])
        mv = sb("mv", [P, HB, 2])
        nmax = sb("nmax", [P, 2])
        nbias = sb("nbias", [P, 2])
        zsum = sb("zsum", [P, NB])
        dsum = sb("dsum", [P, NB])
        ddiag = sb("ddiag", [P, NB])
        deg = sb("deg", [P, NB])
        dinv = sb("dinv", [P, NB])
        rn = sb("rn", [P, HB])
        rn2 = sb("rn2", [P, HB])
        rs = sb("rs", [P, HB])
        minus_half = sb("minus_half", [P, HB])
        vdeg = sb("vdeg", [P, HB])
        vctx = sb("vctx", [P, HB])
        vx1 = sb("vx1", [P, HB])
        vfin = sb("vfin", [P, HB])
        sctx = sb("sctx", [P, HB])
        sx1 = sb("sx1", [P, HB])
        sfin = sb("sfin", [P, HB])

        ps_u = pb("ps_u", [P, N])
        ps_d = pb("ps_d", [P, 2, HALF])
        ps_a = pb("ps_a", [P, 2, HALF])
        ps_acc = pb("ps_acc", [P, HALF])
        ps_n = pb("ps_n", [P, HALF])

        const_in = sem("const_in")
        const_gp = sem("const_gp")
        const_t = sem("const_t")
        bcast_in = sem("bcast_in")
        const_hi = sem("const_hi")
        const_ok = sem("const_ok")
        x_in = sem("x_in")
        xres_in = sem("xres_in")
        a_in = [sem(f"a_in{i}") for i in range(NB)]
        xt_tr = sem("xt_tr")
        xt_hi = sem("xt_hi")
        xt_split = sem("xt_split")
        u_ready = sem("u_ready")
        nmax_ready = sem("nmax_ready")
        nbias_ready = sem("nbias_ready")
        exp_done = sem("exp_done")
        d_ready = sem("d_ready")
        diag_done = sem("diag_done")
        dt_tr = sem("dt_tr")
        dt_hi = sem("dt_hi")
        dt_split = sem("dt_split")
        mask_done = sem("mask_done")
        at_tr = sem("at_tr")
        at_done = sem("at_done")
        h_ready = sem("h_ready")
        h_high = sem("h_high")
        h_split = sem("h_split")
        fold_step = sem("fold_step")
        deg_done = sem("deg_done")
        ctx_done = sem("ctx_done")
        ctxT_ready = sem("ctxT_ready")
        back_ready = sem("back_ready")
        back_read = sem("back_read")
        self_done = sem("self_done")
        post0 = sem("post0")
        norm0 = sem("norm0")
        dinv_ready = sem("dinv_ready")
        vctx_ready = sem("vctx_ready")
        vctx_pow = sem("vctx_pow")
        vx1_ready = sem("vx1_ready")
        vx1_pow = sem("vx1_pow")
        vfin_ready = sem("vfin_ready")
        vfin_pow = sem("vfin_pow")
        x1_ready = sem("x1_ready")
        x1p_ready = sem("x1p_ready")
        x1b_ready = sem("x1b_ready")
        y_done = sem("y_done")
        yT_ready = sem("yT_ready")
        o_ready = sem("o_ready")
        o_read = sem("o_read")
        post1 = sem("post1")
        fin_ready = sem("fin_ready")
        out_done = [sem(f"out_done{h}") for h in range(2)]
        N_CONST = 10

        def rows_of(t, b, r0, r1):
            return t[b if isinstance(b, int) else bass.ds(b, 1), r0:r1, :]

        def batch_rows(t, b, r0, r1):
            v = t[bass.ds(b, 1), r0:r1, :]
            return v.rearrange("o (j p) h -> p (o j) h", p=P)

        def block_rows(t, b, i):
            return t[bass.ds(b, 1), i * P:(i + 1) * P, :].rearrange("o p m -> (o p) m")

        block = ctx.enter_context(nc.Block())

        @block.sync
        def _(sp):
            for k, w in enumerate((Wl, Wr, Ws)):
                sp.dma_start(wraw[:, k, :], w).then_inc(const_in, 16)
            sp.wait_ge(const_gp, 1)
            for k, v in enumerate((bl, br, bs)):
                for row in (0, 32):
                    sp.dma_start(brow[row:row + 1, k * H:(k + 1) * H],
                                 v.rearrange("(a n) -> a n", a=1)).then_inc(const_in, 16)
            sp.dma_start(w1_sb[:, :], W1).then_inc(const_in, 16)

            def load_a(b, i):
                g = NB * b + i
                wait(sp, at_tr, 2 * (g - NB + 1))
                sp.dma_start(a_rows[:, i, :], block_rows(adj, b, i)).then_inc(a_in[i], 16)

            def load_x(b):
                wait(sp, xt_tr, 2 * b)
                sp.dma_start(x_rows[:, :, :], batch_rows(x, b, 0, N)).then_inc(x_in, 16)

            def load_xres(b):
                wait(sp, x1_ready, 2 * b)
                sp.dma_start(x_res[:, :, :], batch_rows(x, b, 0, N)).then_inc(xres_in, 16)

            load_x(0)
            for i in range(NB):
                load_a(0, i)
            load_xres(0)
            with sp.Fori(1, B) as b:
                load_x(b)
                for i in range(NB):
                    if i == 4:
                        load_xres(b)
                    load_a(b, i)

        @block.tensor
        def _(pe):
            def split_matmul(o, hi_l, lo_l, hi_r, lo_r, start, stop):
                pe.matmul(o, hi_l, hi_r, start=start, stop=False)
                pe.matmul(o, hi_l, lo_r, start=False, stop=False)
                return pe.matmul(o, lo_l, hi_r, start=False, stop=stop)

            def turn_x(b):
                pe.wait_ge(x_in, 16 * (b + 1))
                for k in range(2):
                    if isinstance(b, int):
                        pe.wait_ge(const_ok, 1)
                    else:
                        wait(pe, at_done, 2 * (NB * (b - 1) + 4) + 2)
                    for j in range(HB):
                        last = pe.transpose(ps_a[:, k, j * P:(j + 1) * P],
                                            x_rows[:, HB * k + j, :], ident[:, :])
                    last.then_inc(xt_tr, 1)

            def scores(b, i):
                g = NB * b + i
                pe.wait_ge(xt_split, 2 * (b + 1))
                wait(pe, exp_done, g)
                s = slice(i * P, (i + 1) * P)
                for k in range(2):
                    c = slice(k * HALF, (k + 1) * HALF)
                    last = split_matmul(ps_u[:, c], xT_hi[:, s], xT_lo[:, s],
                                        xT_hi[:, c], xT_lo[:, c], True, True)
                last.then_inc(u_ready, 1)

            def project(b):
                pe.wait_ge(xt_split, 2 * (b + 1))
                for j in range(NB):
                    if j < 2:
                        if not isinstance(b, int):
                            wait(pe, at_done, 2 * (NB * (b - 1) + 5) + 2)
                    else:
                        wait(pe, h_split, NB * b + j - 1)
                    o = ps_a[:, j % 2, 0:3 * H]
                    s = slice(j * P, (j + 1) * P)
                    pe.matmul(o, ones[:, :], bias2[:, :], start=True, stop=False)
                    split_matmul(o, xT_hi[:, s], xT_lo[:, s], wT_hi[:, :], wT_lo[:, :],
                                 False, True).then_inc(h_ready, 1)

            def turn_d(b, i):
                g = NB * b + i
                pe.wait_ge(d_ready, g + 1)
                for k in range(2):
                    wait(pe, dt_split, 2 * (g - 1) + k + 1)
                    for j in range(HB):
                        c = (HB * k + j) * P
                        last = pe.transpose(ps_d[:, k, j * P:(j + 1) * P],
                                            d_rows[:, i % 2, c:c + P], ident[:, :])
                    last.then_inc(dt_tr, 1)

            def turn_a(b, i, after_x=None, after_h=None):
                g = NB * b + i
                pe.wait_ge(a_in[i], 16 * (b + 1))
                pe.wait_ge(deg_done, g + 1)
                if after_x is not None:
                    pe.wait_ge(xt_split, 2 * (after_x + 1))
                if after_h is not None:
                    pe.wait_ge(h_split, NB * (after_h + 1))
                for k in range(2):
                    wait(pe, at_done, 2 * (g - 1) + k + 1)
                    for j in range(HB):
                        c = (HB * k + j) * P
                        last = pe.transpose(ps_a[:, k, j * P:(j + 1) * P],
                                            a_rows[:, i, c:c + P], ident[:, :])
                    last.then_inc(at_tr, 1)

            def context(b, half):
                g = NB * b + HB * half
                pe.wait_ge(dt_split, 2 * (g + HB))
                pe.wait_ge(mask_done, 2 * (g + HB))
                pe.wait_ge(h_split, NB * (b + 1))
                if half:
                    pe.wait_ge(ctxT_ready, 2 * b + 1)
                else:
                    wait(pe, yT_ready, 2 * b)
                far = range(HB, NB) if half == 0 else range(0, HB)
                L, R = slice(0, H), slice(H, 2 * H)
                side = L if half == 0 else R
                for j in far:
                    c = slice(0, HALF)
                    split_matmul(ps_acc[:, :], h_hi[:, j, side], h_lo[:, j, side],
                                 dT_hi[:, j, c], dT_lo[:, j, c], j == far[0], False)
                for jj in range(HB):
                    j = HB * half + jj
                    mid = (jj + 1) * P
                    split_matmul(ps_acc[:, 0:mid], h_hi[:, j, L], h_lo[:, j, L],
                                 dT_hi[:, j, 0:mid], dT_lo[:, j, 0:mid], False, False)
                    last = split_matmul(ps_acc[:, mid - P:HALF], h_hi[:, j, R], h_lo[:, j, R],
                                        dT_hi[:, j, mid:], dT_lo[:, j, mid:], False, jj == HB - 1)
                last.then_inc(ctx_done, 1)

            def turn_back(b, half):
                pe.wait_ge(ctxT_ready, 2 * b + half + 1)
                if half:
                    pe.wait_ge(back_read, 2 * b + 1)
                else:
                    wait(pe, o_read, 2 * b)
                for j in range(HB):
                    last = pe.transpose(ps_n[:, j * P:(j + 1) * P], ctxT[:, j * P:(j + 1) * P],
                                        ident[:, :])
                last.then_inc(back_ready, 1)

            def gather(b, half):
                pe.wait_ge(at_done, 2 * NB * (b + 1))
                pe.wait_ge(x1p_ready, 2 * (b + 1))
                if half:
                    pe.wait_ge(yT_ready, 2 * b + 1)
                else:
                    pe.wait_ge(ctxT_ready, 2 * (b + 1))
                for j in range(NB):
                    last = pe.matmul(ps_acc[:, :], x1p[:, j, :],
                                     aT[:, j, half * HALF:(half + 1) * HALF],
                                     start=j == 0, stop=j == NB - 1)
                last.then_inc(y_done, 1)

            def second_product(b, half):
                pe.wait_ge(yT_ready, 2 * b + half + 1)
                if half:
                    pe.wait_ge(o_read, 2 * b + 1)
                else:
                    pe.wait_ge(back_read, 2 * (b + 1))
                for j in range(HB):
                    last = pe.matmul(ps_n[:, j * P:(j + 1) * P], yT[:, half, j * P:(j + 1) * P],
                                     w1_sb[:, :], start=True, stop=True)
                last.then_inc(o_ready, 1)

            def second_layer(b):
                gather(b, 0)
                gather(b, 1)
                second_product(b, 0)
                second_product(b, 1)

            def batch(b, prev):
                turn_x(b)
                scores(b, 0)
                if prev:
                    turn_d(b - 1, NB - 1)
                    turn_a(b - 1, 5, after_x=b)
                    context(b - 1, 1)
                project(b)
                for i in range(NB - 1):
                    scores(b, i + 1)
                    turn_d(b, i)
                    if i == 0 and prev:
                        turn_back(b - 1, 1)
                        turn_a(b - 1, 6, after_h=b)
                    if i == 1 and prev:
                        turn_a(b - 1, 7)
                        second_layer(b - 1)
                    if i == 4:
                        turn_back(b, 0)
                    if i >= 2:
                        turn_a(b, i - 2, after_h=None if prev else b)
                    if i == 3:
                        context(b, 0)

            pe.wait_ge(const_gp, 9)
            pe.wait_ge(const_in, 16 * N_CONST)
            for k in range(3):
                last = pe.transpose(ps_a[:, 0, k * H:(k + 1) * H], wraw[:, k, :], ident[:, :])
            last.then_inc(const_t, 1)
            batch(0, False)
            with pe.Fori(1, B) as b:
                batch(b, True)
            e = B - 1
            turn_d(e, NB - 1)
            turn_a(e, 5)
            context(e, 1)
            turn_a(e, 6)
            turn_back(e, 1)
            turn_a(e, 7)
            second_layer(e)

        @block.scalar
        def _(act):
            for t, v in ((lnw_bc, ln_w), (lnb_bc, ln_b), (b1_bc, b1)):
                act.dma_start(t[:, :], v.partition_broadcast(P)).then_inc(bcast_in, 16)
            act.wait_ge(const_t, 1)
            act.wait_ge(const_in, 16 * N_CONST)
            act.activation(wT_hi[:, :], ps_a[:, 0, 0:3 * H], ACT.Copy).then_inc(const_hi, 1)
            act.activation(brow_hi[:, :], brow[:, :], ACT.Copy).then_inc(const_hi, 1)

            def x_high(b):
                for k in range(2):
                    act.wait_ge(xt_tr, 2 * b + k + 1)
                    wait(act, u_ready, NB * b)
                    wait(act, h_ready, NB * b)
                    act.activation(xT_hi[:, k * HALF:(k + 1) * HALF], ps_a[:, k, :], ACT.Copy)\
                       .then_inc(xt_hi, 1)

            def exps(b, i):
                g = NB * b + i
                act.wait_ge(nbias_ready, g + 1)
                wait(act, d_ready, g - 1)
                act.activation(e_rows[:, i % 2, :], ps_u[:, :], ACT.Exp, bias=nbias[:, i % 2:i % 2 + 1],
                               scale=SCALE, accum_out=zsum[:, i:i + 1]).then_inc(exp_done, 1)

            def d_high(b, i):
                g = NB * b + i
                half, ii = i // HB, i % HB
                wait(act, ctx_done, 2 * b + half)
                for k in range(2):
                    act.wait_ge(dt_tr, 2 * g + k + 1)
                    src = ps_d[:, k, :].rearrange("p (j c) -> p j c", c=P)
                    if k == half:
                        act.activation(dT_hi[:, HB * k + ii:HB * k + HB, ii * P:(ii + 1) * P],
                                       src[:, ii:HB, :], ACT.Copy)
                        last = act.activation(dT_hi[:, HB * k:HB * k + ii + 1, (ii + 1) * P:(ii + 2) * P],
                                              src[:, 0:ii + 1, :], ACT.Copy)
                    else:
                        last = act.activation(dT_hi[:, HB * k:HB * k + HB, ii * P:(ii + 1) * P],
                                              src, ACT.Copy)
                    last.then_inc(dt_hi, 1)

            def a_out(b, i):
                g = NB * b + i
                if i == 0:
                    wait(act, y_done, 2 * b)
                for k in range(2):
                    act.wait_ge(at_tr, 2 * g + k + 1)
                    act.activation(aT[:, HB * k:HB * k + HB, i * P:(i + 1) * P],
                                   ps_a[:, k, :].rearrange("p (j c) -> p j c", c=P), ACT.Copy)\
                       .then_inc(at_done, 1)

            def h_parts(b):
                wait(act, ctx_done, 2 * b)
                for j in range(NB):
                    act.wait_ge(h_ready, NB * b + j + 1)
                    act.activation(h_hi[:, j, :], ps_a[:, j % 2, 0:2 * H], ACT.Copy)\
                       .then_inc(h_high, 1)

            def ctx_out(b, half):
                act.wait_ge(ctx_done, 2 * b + half + 1)
                wait(act, back_ready, 2 * b + half)
                act.activation(ctxT[:, :], ps_acc[:, :], ACT.Copy).then_inc(ctxT_ready, 1)

            def y_out(b, half):
                act.wait_ge(y_done, 2 * b + half + 1)
                act.activation(yT[:, half, :], ps_acc[:, :], ACT.Copy).then_inc(yT_ready, 1)

            def batch(b, prev):
                x_high(b)
                exps(b, 0)
                if prev:
                    d_high(b - 1, NB - 1)
                    a_out(b - 1, 5)
                    ctx_out(b - 1, 1)
                h_parts(b)
                for i in range(NB - 1):
                    exps(b, i + 1)
                    d_high(b, i)
                    if i == 0 and prev:
                        a_out(b - 1, 6)
                    if i == 1 and prev:
                        a_out(b - 1, 7)
                        y_out(b - 1, 0)
                        y_out(b - 1, 1)
                    if i >= 2:
                        a_out(b, i - 2)
                    if i == 3:
                        ctx_out(b, 0)

            batch(0, False)
            with act.Fori(1, B) as b:
                batch(b, True)
            e = B - 1
            d_high(e, NB - 1)
            a_out(e, 5)
            ctx_out(e, 1)
            a_out(e, 6)
            a_out(e, 7)
            y_out(e, 0)
            y_out(e, 1)

        @block.vector
        def _(dve):
            def f(t):
                return t.bitcast(F32)

            dve.wait_ge(const_hi, 2)
            dve.tensor_tensor(wT_lo[:, :], ps_a[:, 0, 0:3 * H], f(wT_hi[:, :]), ALU.subtract)
            dve.wait_ge(const_gp, 9)
            dve.tensor_copy(bias2[0:1, :], f(brow_hi[0:1, :]))
            dve.tensor_tensor(bias2[32:33, :], brow[32:33, :], f(brow_hi[32:33, :]), ALU.subtract)
            dve.tensor_copy(ones[:, :], onesf[:, :]).then_inc(const_ok, 1)

            def x_low(b):
                for k in range(2):
                    dve.wait_ge(xt_hi, 2 * b + k + 1)
                    c = slice(k * HALF, (k + 1) * HALF)
                    dve.tensor_tensor(xT_lo[:, c], ps_a[:, k, :], f(xT_hi[:, c]), ALU.subtract)\
                       .then_inc(xt_split, 1)

            def row_max(b, i):
                g = NB * b + i
                s = slice(i % 2, i % 2 + 1)
                dve.wait_ge(u_ready, g + 1)
                dve.tensor_reduce(nmax[:, s], ps_u[:, :], AX.X, ALU.max, negate=True).then_inc(nmax_ready, 1)
                dve.wait_ge(nmax_ready, g + 1)
                dve.tensor_scalar(nbias[:, s], nmax[:, s], SCALE, None, ALU.mult).then_inc(nbias_ready, 1)

            def masked(b, i):
                g = NB * b + i
                dve.wait_ge(exp_done, g + 1)
                dve.wait_ge(a_in[i], 16 * (b + 1))
                wait(dve, dt_tr, 2 * (g - 1))
                dve.tensor_tensor_reduce(out=d_rows[:, i % 2, :], in0=e_rows[:, i % 2, :],
                                         in1=a_rows[:, i, :], scale=1.0, scalar=0.0, op0=ALU.mult,
                                         op1=ALU.add, accum_out=dsum[:, i:i + 1]).then_inc(d_ready, 1)

            def finish_d(b, i):
                g = NB * b + i
                half, ii = i // HB, i % HB
                dve.wait_ge(d_ready, g + 1)
                dve.wait_ge(diag_done, g) if not (isinstance(g, int) and g == 0) else None
                dve.tensor_tensor_reduce(out=junk[:, :], in0=d_rows[:, i % 2, i * P:(i + 1) * P],
                                         in1=ident[:, :], scale=1.0, scalar=0.0, op0=ALU.mult,
                                         op1=ALU.add, accum_out=ddiag[:, i:i + 1]).then_inc(diag_done, 1)
                for k in range(2):
                    dve.wait_ge(dt_hi, 2 * g + k + 1)
                    src = ps_d[:, k, :].rearrange("p (j c) -> p j c", c=P)
                    if k == half:
                        a = (slice(None), slice(HB * k + ii, HB * k + HB), slice(ii * P, (ii + 1) * P))
                        c = (slice(None), slice(HB * k, HB * k + ii + 1), slice((ii + 1) * P, (ii + 2) * P))
                        dve.tensor_tensor(dT_lo[a], src[:, ii:HB, :], f(dT_hi[a]), ALU.subtract)
                        last = dve.tensor_tensor(dT_lo[c], src[:, 0:ii + 1, :], f(dT_hi[c]), ALU.subtract)
                    else:
                        a = (slice(None), slice(HB * k, HB * k + HB), slice(ii * P, (ii + 1) * P))
                        last = dve.tensor_tensor(dT_lo[a], src, f(dT_hi[a]), ALU.subtract)
                    last.then_inc(dt_split, 1)
                dve.wait_ge(fold_step, 3 * (g + 1))
                dve.tensor_reduce(deg[:, i:i + 1], fold3[:, :], AX.X, ALU.add).then_inc(deg_done, 1)

            def h_low(b):
                for j in range(NB):
                    dve.wait_ge(h_high, NB * b + j + 1)
                    dve.tensor_tensor(h_lo[:, j, :], ps_a[:, j % 2, 0:2 * H], f(h_hi[:, j, :]), ALU.subtract)
                    dve.tensor_copy(h_self[:, j, :], ps_a[:, j % 2, 2 * H:3 * H]).then_inc(h_split, 1)

            def self_term(b, half):
                n = 2 * b + half
                wait(dve, norm0, 3 * n)
                dve.wait_ge(diag_done, NB * b + HB * (half + 1))
                for k in range(HB):
                    i = HB * half + k
                    last = dve.tensor_scalar(c_rows[:, k, :], h_self[:, i, :], ddiag[:, i:i + 1], None,
                                             ALU.mult)
                last.then_inc(self_done, 1)

            def after_context(b, half):
                n = 2 * b + half
                base = 9 * n
                cols = slice(HB * half, HB * (half + 1))
                if half == 0:
                    for k in range(2):
                        wait(dve, out_done[k], 16 * b)
                    self_term(b, 0)
                dve.wait_ge(back_ready, n + 1)
                dve.wait_ge(self_done, n + 1)
                dve.tensor_tensor(c_rows[:, :, :], ps_n[:, :].rearrange("p (k h) -> p k h", h=H),
                                  c_rows[:, :, :], ALU.add).then_inc(back_read, 1)
                dve.scalar_tensor_tensor(out=rn2[:, :], in0=zsum[:, cols], scalar=EPS_RENORM,
                                         in1=dsum[:, cols], op0=ALU.mult, op1=ALU.add).then_inc(post0, 1)
                dve.wait_ge(post0, base + 1)
                dve.reciprocal(rn[:, :], rn2[:, :]).then_inc(post0, 1)
                dve.wait_ge(back_read, n + 1)
                for k in range(HB):
                    last = dve.bn_stats(stats[:, k, :], c_rows[:, k, :])
                last.then_inc(post0, 1)
                dve.wait_ge(post0, base + 3)
                dve.tensor_tensor(rn2[:, :], rn[:, :], rn[:, :], ALU.mult)
                for k in range(HB):
                    last = dve.bn_aggr(mv[:, k, :], stats[:, k, :])
                last.then_inc(post0, 1)
                dve.wait_ge(post0, base + 4)
                dve.tensor_tensor(rs[:, :], mv[:, :, 1], rn2[:, :], ALU.mult).then_inc(post0, 1)
                dve.wait_ge(post0, base + 5)
                dve.tensor_scalar(vctx[:, :], rs[:, :], EPS_CTX, None, ALU.add).then_inc(vctx_ready, 1)
                dve.wait_ge(vctx_pow, n + 1)
                dve.tensor_tensor(rs[:, :], sctx[:, :], rn[:, :], ALU.mult).then_inc(post0, 1)
                dve.wait_ge(post0, base + 6)
                for k in range(HB):
                    last = dve.tensor_scalar(c_rows[:, k, :], c_rows[:, k, :], mv[:, k, 0:1], rs[:, k:k + 1],
                                             ALU.subtract, ALU.mult)
                last.then_inc(norm0, 1)
                dve.wait_ge(norm0, 3 * n + 3)
                dve.wait_ge(xres_in, 16 * (b + 1))
                dve.scalar_tensor_tensor(out=c_rows[:, :, :], in0=c_rows[:, :, :], scalar=0.0,
                                         in1=x_res[:, cols, :], op0=ALU.max, op1=ALU.add).then_inc(post0, 1)
                dve.wait_ge(post0, base + 7)
                for k in range(HB):
                    last = dve.bn_stats(stats[:, k, :], c_rows[:, k, :])
                last.then_inc(post0, 1)
                dve.wait_ge(post0, base + 8)
                dve.tensor_scalar(vdeg[:, :], deg[:, cols], EPS_DEG, None, ALU.add)
                for k in range(HB):
                    last = dve.bn_aggr(mv[:, k, :], stats[:, k, :])
                last.then_inc(post0, 1)
                dve.wait_ge(post0, base + 9)
                dve.tensor_scalar(vx1[:, :], mv[:, :, 1], EPS_LN, None, ALU.add).then_inc(vx1_ready, 1)
                dve.wait_ge(vx1_pow, n + 1)
                for k in range(HB):
                    last = dve.tensor_scalar(x1[:, HB * half + k, :], c_rows[:, k, :], mv[:, k, 0:1],
                                             sx1[:, k:k + 1], ALU.subtract, ALU.mult)
                last.then_inc(x1_ready, 1)

            def after_product(b, half):
                n = 2 * b + half
                base = 4 * n
                dve.wait_ge(o_ready, n + 1)
                dve.wait_ge(dinv_ready, 2 * (b + 1))
                dve.wait_ge(x1b_ready, n + 1)
                for k in range(HB):
                    i = HB * half + k
                    last = dve.scalar_tensor_tensor(out=fin[:, half, k, :], in0=ps_n[:, k * P:(k + 1) * P],
                                                    scalar=dinv[:, i:i + 1], in1=x1b[:, i, :],
                                                    op0=ALU.mult, op1=ALU.add)
                last.then_inc(o_read, 1)
                dve.wait_ge(o_read, n + 1)
                for k in range(HB):
                    last = dve.bn_stats(stats[:, k, :], fin[:, half, k, :])
                last.then_inc(post1, 1)
                dve.wait_ge(post1, base + 1)
                dve.sem_inc(post1, 1)
                for k in range(HB):
                    last = dve.bn_aggr(mv[:, k, :], stats[:, k, :])
                last.then_inc(post1, 1)
                dve.wait_ge(post1, base + 3)
                dve.tensor_scalar(vfin[:, :], mv[:, :, 1], EPS_LN, None, ALU.add).then_inc(vfin_ready, 1)
                dve.wait_ge(vfin_pow, n + 1)
                for k in range(HB):
                    last = dve.tensor_scalar(fin[:, half, k, :], fin[:, half, k, :], mv[:, k, 0:1],
                                             sfin[:, k:k + 1], ALU.subtract, ALU.mult)
                last.then_inc(post1, 1)

            def batch(b, prev):
                if prev:
                    masked(b - 1, NB - 1)
                x_low(b)
                row_max(b, 0)
                if prev:
                    finish_d(b - 1, NB - 1)
                    self_term(b - 1, 1)
                h_low(b)
                for i in range(NB - 1):
                    masked(b, i)
                    if i == 2 and prev:
                        after_product(b - 1, 0)
                        after_product(b - 1, 1)
                    row_max(b, i + 1)
                    finish_d(b, i)
                    if i == 0 and prev:
                        after_context(b - 1, 1)
                    if i == 4:
                        after_context(b, 0)

            batch(0, False)
            with dve.Fori(1, B) as b:
                batch(b, True)
            e = B - 1
            masked(e, NB - 1)
            finish_d(e, NB - 1)
            self_term(e, 1)
            after_context(e, 1)
            after_product(e, 0)
            after_product(e, 1)

        @block.gpsimd
        def _(pool):
            pool.memset(brow[:, :], 0.0).then_inc(const_gp, 1)
            pool.memset(ident[:, :], 0.0).then_inc(const_gp, 1)
            pool.memset(onesf[:, :], 1.0).then_inc(const_gp, 1)
            pool.memset(bias2[:, :].bitcast(F32), 0.0).then_inc(const_gp, 1)
            pool.memset(sides[:, :], 1.0).then_inc(const_gp, 1)
            pool.memset(minus_half[:, :], -0.5).then_inc(const_gp, 1)
            pool.wait_ge(const_gp, 6)
            pool.affine_select(out=ident[:, :], in_=ident[:, :], compare_op=ALU.not_equal, fill=1.0,
                               base=0, pattern=[[-1, P]], channel_multiplier=1).then_inc(const_gp, 1)
            for k, sign in ((0, 1), (1, -1)):
                v = sides[:, k * P:(k + 1) * P]
                pool.affine_select(out=v, in_=v, compare_op=ALU.is_gt, fill=0.0, base=0,
                                   pattern=[[-sign, P]], channel_multiplier=sign).then_inc(const_gp, 1)
            pool.wait_ge(const_gp, 9)
            pool.wait_ge(bcast_in, 48)

            def fold_a(b, i):
                g = NB * b + i
                pool.wait_ge(a_in[i], 16 * (b + 1))
                pool.tensor_tensor(fold[:, :], a_rows[:, i, 0:HALF], a_rows[:, i, HALF:N], ALU.add)\
                    .then_inc(fold_step, 1)
                pool.wait_ge(fold_step, 3 * g + 1)
                pool.tensor_tensor(fold2[:, :], fold[:, 0:HALF // 2], fold[:, HALF // 2:HALF], ALU.add)\
                    .then_inc(fold_step, 1)
                pool.wait_ge(fold_step, 3 * g + 2)
                wait(pool, deg_done, g)
                pool.tensor_tensor(fold3[:, :], fold2[:, 0:P], fold2[:, P:2 * P], ALU.add)\
                    .then_inc(fold_step, 1)

            def masks(b, i):
                g = NB * b + i
                half, ii = i // HB, i % HB
                pool.wait_ge(dt_split, 2 * g + half + 1)
                for t in (dT_hi, dT_lo):
                    v = t[:, i, ii * P:(ii + 2) * P]
                    pool.tensor_tensor(v, v.bitcast(F32), sides[:, :], ALU.mult).then_inc(mask_done, 1)

            def affine(b, half):
                n = 2 * b + half
                cols = slice(HB * half, HB * (half + 1))

                def bc(t):
                    return t[:, :].rearrange("p (a h) -> p a h", a=1).to_broadcast([P, HB, H])

                pool.wait_ge(vctx_ready, n + 1)
                pool.tensor_tensor(sctx[:, :], vctx[:, :], minus_half[:, :], ALU.pow).then_inc(vctx_pow, 1)
                pool.wait_ge(norm0, 3 * n + 1)
                pool.tensor_tensor(c_rows[:, :, :], c_rows[:, :, :], bc(lnw_bc), ALU.mult).then_inc(norm0, 1)
                pool.wait_ge(norm0, 3 * n + 2)
                pool.tensor_tensor(c_rows[:, :, :], c_rows[:, :, :], bc(lnb_bc), ALU.add).then_inc(norm0, 1)
                pool.wait_ge(vx1_ready, n + 1)
                pool.tensor_tensor(sx1[:, :], vx1[:, :], minus_half[:, :], ALU.pow).then_inc(vx1_pow, 1)
                pool.tensor_tensor(dinv[:, cols], vdeg[:, :], minus_half[:, :], ALU.pow).then_inc(dinv_ready, 1)
                pool.wait_ge(x1_ready, n + 1)
                pool.wait_ge(dinv_ready, n + 1)
                if half == 0:
                    wait(pool, y_done, 2 * b)
                    wait(pool, o_read, 2 * b)
                pool.tensor_tensor(x1p[:, cols, :], x1[:, cols, :],
                                   dinv[:, cols].rearrange("p (j a) -> p j a", a=1).to_broadcast([P, HB, H]),
                                   ALU.mult).then_inc(x1p_ready, 1)
                pool.tensor_tensor(x1b[:, cols, :], x1[:, cols, :], bc(b1_bc), ALU.add).then_inc(x1b_ready, 1)

            def store(b, half):
                n = 2 * b + half
                pool.wait_ge(vfin_ready, n + 1)
                pool.tensor_tensor(sfin[:, :], vfin[:, :], minus_half[:, :], ALU.pow).then_inc(vfin_pow, 1)
                pool.wait_ge(post1, 4 * (n + 1))
                pool.dma_start(batch_rows(out, b, half * HALF, (half + 1) * HALF), fin[:, half, :, :])\
                    .then_inc(out_done[half], 16)

            def batch(b, prev):
                if prev:
                    masks(b - 1, NB - 1)
                for i in range(NB - 1):
                    fold_a(b, i)
                    if i == 2 and prev:
                        store(b - 1, 0)
                        store(b - 1, 1)
                    masks(b, i)
                    if i == 0 and prev:
                        affine(b - 1, 1)
                    if i == 4:
                        affine(b, 0)
                fold_a(b, NB - 1)

            batch(0, False)
            with pool.Fori(1, B) as b:
                batch(b, True)
            e = B - 1
            masks(e, NB - 1)
            affine(e, 1)
            store(e, 0)
            store(e, 1)
            for half in range(2):
                pool.wait_ge(out_done[half], 16 * B)


_INS = ['x', 'adj', 'L0_gnn_Wl', 'L0_gnn_bl', 'L0_gnn_Ws', 'L0_gnn_bs', 'L0_gnn_Wr', 'L0_gnn_br',
        'L0_gnn_ln_w', 'L0_gnn_ln_b', 'L1_gnn_weight', 'L1_gnn_bias']


def kernel(**inputs):
    import numpy as _np
    import concourse.bacc as _bacc
    from concourse import mybir as _mybir
    from concourse.bass_utils import run_bass_kernel_spmd as _run

    nc = _bacc.Bacc("TRN2", target_bir_lowering=False, num_devices=1)
    arrays, args = {}, []
    for name in _INS:
        a = _np.ascontiguousarray(inputs[name])
        arrays[f"in_{name}_dram"] = a
        args.append(nc.dram_tensor(f"in_{name}_dram", a.shape, _mybir.dt.from_np(a.dtype), kind="ExternalInput").ap())
    shape = arrays["in_x_dram"].shape
    args.append(nc.dram_tensor("out_0_dram", shape, _mybir.dt.float32, kind="ExternalOutput").ap())
    two_layer_graph_kernel(nc, *args)
    r = _run(nc, [arrays], core_ids=[0])
    return r.results[0]["out_0_dram"]
```

```python
from contextlib import ExitStack

import concourse.bass as bass
from concourse import mybir

F32 = mybir.dt.float32
F32R = mybir.dt.float32r
ALU = mybir.AluOpType
ACT = mybir.ActivationFunctionType
AX = mybir.AxisListType

P = 128
EPS_RENORM = 1e-10
EPS_CTX = 1e-12
EPS_LN = 1e-5
EPS_DEG = 1e-5


def wait(eng, sem, value):
    if isinstance(value, int) and value <= 0:
        return
    eng.wait_ge(sem, value)


def two_layer_graph_kernel(nc, x, adj, Wl, bl, Ws, bs, Wr, br, ln_w, ln_b, W1, b1, out):
    B, N, H = x.shape
    NB = N // P
    HB = NB // 2
    HALF = N // 2
    SCALE = float(H) ** -0.5
    assert H == P and NB == 8 and HALF == 512

    with ExitStack() as ctx:
        def sb(name, shape, dt=F32):
            return ctx.enter_context(nc.sbuf_tensor(name, shape, dt))

        def pb(name, shape):
            return ctx.enter_context(nc.psum_tensor(name, shape, F32))

        def sem(name):
            return ctx.enter_context(nc.semaphore(name))

        ident = sb("ident", [P, P])
        ones = sb("ones", [64, P], F32R)
        onesf = sb("onesf", [64, P])
        sides = sb("sides", [P, 2 * P])
        wraw = sb("wraw", [P, 3, H])
        wT_hi = sb("wT_hi", [P, 3 * H], F32R)
        wT_lo = sb("wT_lo", [P, 3 * H], F32R)
        brow = sb("brow", [64, 3 * H])
        brow_hi = sb("brow_hi", [64, 3 * H], F32R)
        bias2 = sb("bias2", [64, 3 * H], F32R)
        w1_sb = sb("w1_sb", [P, H])
        lnw_bc = sb("lnw_bc", [P, H])
        lnb_bc = sb("lnb_bc", [P, H])
        b1_bc = sb("b1_bc", [P, H])

        x_rows = sb("x_rows", [P, NB, H])
        x_res = sb("x_res", [P, NB, H])
        xT_hi = sb("xT_hi", [P, N], F32R)
        xT_lo = sb("xT_lo", [P, N], F32R)
        h_hi = sb("h_hi", [P, NB, 2 * H], F32R)
        h_lo = sb("h_lo", [P, NB, 2 * H], F32R)
        h_self = sb("h_self", [P, NB, H])
        a_rows = sb("a_rows", [P, NB, N])
        aT = sb("aT", [P, NB, N])
        e_rows = sb("e_rows", [P, 2, N])
        d_rows = sb("d_rows", [P, 2, N])
        dT_hi = sb("dT_hi", [P, NB, HALF + P], F32R)
        dT_lo = sb("dT_lo", [P, NB, HALF + P], F32R)
        ctxT = sb("ctxT", [P, HALF])
        yT = sb("yT", [P, 2, HALF])
        c_rows = sb("c_rows", [P, 2, HB, H])
        x1 = sb("x1", [P, NB, H])
        x1p = sb("x1p", [P, NB, H])
        x1b = sb("x1b", [P, NB, H])
        fin = sb("fin", [P, 2, HB, H])
        junk = sb("junk", [P, P])
        junk_a = sb("junk_a", [P, N], mybir.dt.bfloat16)
        nmax = sb("nmax", [P, 2])
        nbias = sb("nbias", [P, 2])
        zsum = sb("zsum", [P, NB])
        dsum = sb("dsum", [P, NB])
        ddiag = sb("ddiag", [P, NB])
        deg = sb("deg", [P, NB])
        dinv = sb("dinv", [P, NB])
        minus_half = sb("minus_half", [P, HB])
        rn = sb("rn", [P, 2, HB])
        rn2 = sb("rn2", [P, 2, HB])
        vdeg = sb("vdeg", [P, 2, HB])
        NORMS = ("c", "x", "f")
        stats = {k: sb(f"stats_{k}", [P, 2, HB, 6]) for k in NORMS}
        mv = {k: sb(f"mv_{k}", [P, 2, HB, 2]) for k in NORMS}
        nmean = {k: sb(f"nmean_{k}", [P, 2, HB]) for k in NORMS}
        var = {k: sb(f"var_{k}", [P, 2, HB]) for k in NORMS}
        power = {k: sb(f"power_{k}", [P, 2, HB]) for k in NORMS}
        scale = {k: sb(f"scale_{k}", [P, 2, HB]) for k in NORMS}
        shift = {k: sb(f"shift_{k}", [P, 2, HB]) for k in NORMS}

        row_scales = {"c": scale["c"], "x": power["x"], "f": power["f"]}

        ps_u = pb("ps_u", [P, N])
        ps_d = pb("ps_d", [P, 2, HALF])
        ps_m = pb("ps_m", [P, 2, HALF])
        ps_acc = pb("ps_acc", [P, 2, HALF])

        const_in = sem("const_in")
        const_gp = sem("const_gp")
        const_t = sem("const_t")
        bcast_in = sem("bcast_in")
        const_hi = sem("const_hi")
        const_ok = sem("const_ok")
        x_in = sem("x_in")
        xres_in = sem("xres_in")
        a_in = [sem(f"a_in{i}") for i in range(NB)]
        xt_tr = sem("xt_tr")
        xt_hi = sem("xt_hi")
        xt_split = sem("xt_split")
        u_ready = sem("u_ready")
        nmax_ready = sem("nmax_ready")
        nbias_ready = sem("nbias_ready")
        exp_done = sem("exp_done")
        d_ready = sem("d_ready")
        diag_done = sem("diag_done")
        dt_tr = sem("dt_tr")
        dt_hi = sem("dt_hi")
        dt_split = sem("dt_split")
        mask_done = sem("mask_done")
        at_tr = sem("at_tr")
        at_done = sem("at_done")
        h_ready = sem("h_ready")
        h_high = sem("h_high")
        hs_ready = sem("hs_ready")
        h_split = sem("h_split")
        deg_done = sem("deg_done")
        ctx_done = sem("ctx_done")
        ctxT_ready = sem("ctxT_ready")
        self_done = sem("self_done")
        back_ready = sem("back_ready")
        back_read = sem("back_read")
        c_step = sem("c_step")
        c_var = sem("c_var")
        c_power = sem("c_power")
        c_scaled = sem("c_scaled")
        x_power = sem("x_power")
        f_power = sem("f_power")
        c_small = sem("c_small")
        c_scale = sem("c_scale")
        c_norm = sem("c_norm")
        affine_w = sem("affine_w")
        affine_b = sem("affine_b")
        x_step = sem("x_step")
        x_var = sem("x_var")
        x_small = sem("x_small")
        x_scale = sem("x_scale")
        dinv_ready = sem("dinv_ready")
        x1_ready = sem("x1_ready")
        x1p_ready = sem("x1p_ready")
        x1b_ready = sem("x1b_ready")
        y_done = sem("y_done")
        yT_ready = sem("yT_ready")
        o_ready = sem("o_ready")
        o_read = sem("o_read")
        f_step = sem("f_step")
        f_var = sem("f_var")
        f_small = sem("f_small")
        f_scale = sem("f_scale")
        f_norm = sem("f_norm")
        out_done = [sem(f"out_done{h}") for h in range(2)]
        N_CONST = 10

        def rows_of(t, b, r0, r1):
            return t[b if isinstance(b, int) else bass.ds(b, 1), r0:r1, :]

        def batch_rows(t, b, r0, r1):
            v = t[bass.ds(b, 1), r0:r1, :]
            return v.rearrange("o (j p) h -> p (o j) h", p=P)

        def block_rows(t, b, i):
            return t[bass.ds(b, 1), i * P:(i + 1) * P, :].rearrange("o p m -> (o p) m")

        block = ctx.enter_context(nc.Block())

        @block.sync
        def _(sp):
            for k, w in enumerate((Wl, Wr, Ws)):
                sp.dma_start(wraw[:, k, :], w).then_inc(const_in, 16)
            sp.wait_ge(const_gp, 1)
            for k, v in enumerate((bl, br, bs)):
                for row in (0, 32):
                    sp.dma_start(brow[row:row + 1, k * H:(k + 1) * H],
                                 v.rearrange("(a n) -> a n", a=1)).then_inc(const_in, 16)
            sp.dma_start(w1_sb[:, :], W1).then_inc(const_in, 16)

            def load_a(b, i):
                g = NB * b + i
                wait(sp, at_tr, 2 * (g - NB + 1))
                sp.dma_start(a_rows[:, i, :], block_rows(adj, b, i)).then_inc(a_in[i], 16)

            def load_x(b):
                wait(sp, xt_tr, 2 * b)
                sp.dma_start(x_rows[:, :, :], batch_rows(x, b, 0, N)).then_inc(x_in, 16)

            def load_xres(b):
                wait(sp, x_step, 3 * 2 * b)
                sp.dma_start(x_res[:, :, :], batch_rows(x, b, 0, N)).then_inc(xres_in, 16)

            load_x(0)
            for i in range(NB):
                load_a(0, i)
            load_xres(0)
            with sp.Fori(1, B) as b:
                load_x(b)
                for i in range(NB):
                    if i == 4:
                        load_xres(b)
                    load_a(b, i)

        @block.tensor
        def _(pe):
            def split_matmul(o, hi_l, lo_l, hi_r, lo_r, start, stop):
                pe.matmul(o, hi_l, hi_r, start=start, stop=False)
                pe.matmul(o, hi_l, lo_r, start=False, stop=False)
                return pe.matmul(o, lo_l, hi_r, start=False, stop=stop)


            def turn_x(b):
                pe.wait_ge(x_in, 16 * (b + 1))
                for k in range(2):
                    if isinstance(b, int):
                        pe.wait_ge(const_ok, 1)
                    else:
                        pe.wait_ge(at_done, 2 * (NB * (b - 1) + 5) + k + 1)
                    for j in range(HB):
                        last = pe.transpose(ps_m[:, k, j * P:(j + 1) * P],
                                            x_rows[:, HB * k + j, :], ident[:, :])
                    last.then_inc(xt_tr, 1)

            def scores(b, i):
                g = NB * b + i
                pe.wait_ge(xt_split, 2 * (b + 1))
                wait(pe, exp_done, g)
                s = slice(i * P, (i + 1) * P)
                for k in range(2):
                    c = slice(k * HALF, (k + 1) * HALF)
                    last = split_matmul(ps_u[:, c], xT_hi[:, s], xT_lo[:, s],
                                        xT_hi[:, c], xT_lo[:, c], True, True)
                last.then_inc(u_ready, 1)

            def project(b):
                pe.wait_ge(xt_split, 2 * (b + 1))
                for j in range(NB):
                    if j == 0 and not isinstance(b, int):
                        pe.wait_ge(at_done, 2 * NB * b)
                    if j == 1 and not isinstance(b, int):
                        pe.wait_ge(back_read, 2 * b)
                    if j >= 2:
                        wait(pe, h_split, NB * b + j - 1)
                    o = ps_m[:, (j + 1) % 2, 0:3 * H]
                    s = slice(j * P, (j + 1) * P)
                    pe.matmul(o, ones[:, :], bias2[:, :], start=True, stop=False)
                    split_matmul(o, xT_hi[:, s], xT_lo[:, s], wT_hi[:, :], wT_lo[:, :],
                                 False, True).then_inc(h_ready, 1)

            def turn_d(b, i):
                g = NB * b + i
                pe.wait_ge(d_ready, g + 1)
                for k in range(2):
                    wait(pe, dt_split, 2 * (g - 1) + k + 1)
                    for j in range(HB):
                        c = (HB * k + j) * P
                        last = pe.transpose(ps_d[:, k, j * P:(j + 1) * P],
                                            d_rows[:, i % 2, c:c + P], ident[:, :])
                    last.then_inc(dt_tr, 1)

            def turn_a(b, i, after_x=None, first=False):
                g = NB * b + i
                pe.wait_ge(a_in[i], 16 * (b + 1))
                pe.wait_ge(d_ready, g + 1)
                pe.wait_ge(deg_done, g + 1)
                for k in range(2):
                    if i == 0:
                        pe.wait_ge(h_split, NB * (b + 1))
                    elif i == 2 and k == 0:
                        pe.wait_ge(back_read, 2 * b + 1)
                    elif i == 2 and not first:
                        pe.wait_ge(o_read, 2 * b)
                    elif after_x is not None:
                        pe.wait_ge(xt_split, 2 * after_x + k + 1)
                    else:
                        pe.wait_ge(at_done, 2 * (g - 1) + k + 1)
                    for j in range(HB):
                        c = (HB * k + j) * P
                        last = pe.transpose(ps_m[:, k, j * P:(j + 1) * P],
                                            a_rows[:, i, c:c + P], ident[:, :])
                    last.then_inc(at_tr, 1)

            def context(b, half):
                g = NB * b + HB * half
                pe.wait_ge(dt_split, 2 * (g + HB))
                pe.wait_ge(mask_done, 2 * (g + HB))
                pe.wait_ge(h_split, NB * (b + 1))
                if half == 0:
                    wait(pe, yT_ready, 2 * b - 1)
                acc = ps_acc[:, half, :]
                far = range(HB, NB) if half == 0 else range(0, HB)
                L, R = slice(0, H), slice(H, 2 * H)
                side = L if half == 0 else R
                for j in far:
                    c = slice(0, HALF)
                    split_matmul(acc, h_hi[:, j, side], h_lo[:, j, side],
                                 dT_hi[:, j, c], dT_lo[:, j, c], j == far[0], False)
                for jj in range(HB):
                    j = HB * half + jj
                    mid = (jj + 1) * P
                    split_matmul(acc[:, 0:mid], h_hi[:, j, L], h_lo[:, j, L],
                                 dT_hi[:, j, 0:mid], dT_lo[:, j, 0:mid], False, False)
                    last = split_matmul(acc[:, mid - P:HALF], h_hi[:, j, R], h_lo[:, j, R],
                                        dT_hi[:, j, mid:], dT_lo[:, j, mid:], False, jj == HB - 1)
                last.then_inc(ctx_done, 1)

            def turn_back(b, half):
                pe.wait_ge(ctxT_ready, 2 * b + half + 1)
                if half:
                    pe.wait_ge(at_done, 2 * NB * (b + 1) - 1)
                elif isinstance(b, int):
                    pe.wait_ge(at_done, 2 * (NB * b + 1) + 1)
                else:
                    pe.wait_ge(o_read, 2 * b - 1)
                for j in range(HB):
                    last = pe.transpose(ps_m[:, 0, j * P:(j + 1) * P], ctxT[:, j * P:(j + 1) * P],
                                        ident[:, :])
                last.then_inc(back_ready, 1)

            def gather(b, half, part):
                pe.wait_ge(at_done, 2 * NB * (b + 1))
                pe.wait_ge(x1p_ready, 2 * b + part + 1)
                if part == 0:
                    pe.wait_ge(ctxT_ready, 2 * b + half + 1)
                for j in range(HB * part, HB * (part + 1)):
                    last = pe.matmul(ps_acc[:, half, :], x1p[:, j, :],
                                     aT[:, j, half * HALF:(half + 1) * HALF],
                                     start=j == 0, stop=j == NB - 1)
                if part:
                    last.then_inc(y_done, 1)

            def second_product(b, half, bank_from):
                pe.wait_ge(yT_ready, 2 * b + half + 1)
                pe.wait_ge(at_done, 2 * bank_from + half + 1)
                for j in range(HB):
                    last = pe.matmul(ps_m[:, half, j * P:(j + 1) * P], yT[:, half, j * P:(j + 1) * P],
                                     w1_sb[:, :], start=True, stop=True)
                last.then_inc(o_ready, 1)

            def batch(b, prev):
                p = b - 1
                turn_x(b)
                if prev:
                    turn_d(p, 7)
                    turn_a(p, 6, after_x=b)
                scores(b, 0)
                if prev:
                    turn_a(p, 7)
                    context(p, 1)
                scores(b, 1)
                if prev:
                    turn_back(p, 1)
                turn_d(b, 0)
                project(b)
                scores(b, 2)
                turn_d(b, 1)
                if prev:
                    gather(p, 0, 0)
                    gather(p, 1, 0)
                scores(b, 3)
                turn_d(b, 2)
                if prev:
                    gather(p, 0, 1)
                scores(b, 4)
                turn_d(b, 3)
                if prev:
                    gather(p, 1, 1)
                turn_a(b, 0)
                turn_a(b, 1)
                context(b, 0)
                scores(b, 5)
                turn_d(b, 4)
                if prev:
                    second_product(p, 0, NB * b + 1)
                    second_product(p, 1, NB * b + 1)
                turn_back(b, 0)
                scores(b, 6)
                turn_d(b, 5)
                turn_a(b, 2, first=not prev)
                scores(b, 7)
                turn_d(b, 6)
                turn_a(b, 3)
                turn_a(b, 4)
                turn_a(b, 5)

            pe.wait_ge(const_gp, 9)
            pe.wait_ge(const_in, 16 * N_CONST)
            for k in range(3):
                last = pe.transpose(ps_m[:, 0, k * H:(k + 1) * H], wraw[:, k, :], ident[:, :])
            last.then_inc(const_t, 1)
            batch(0, False)
            with pe.Fori(1, B) as b:
                batch(b, True)
            e = B - 1
            turn_d(e, 7)
            turn_a(e, 6)
            turn_a(e, 7)
            context(e, 1)
            turn_back(e, 1)
            for part in range(2):
                for half in range(2):
                    gather(e, half, part)
            for half in range(2):
                second_product(e, half, NB * e + 7)

        @block.scalar
        def _(act):
            for t, v in ((lnw_bc, ln_w), (lnb_bc, ln_b), (b1_bc, b1)):
                act.dma_start(t[:, :], v.partition_broadcast(P)).then_inc(bcast_in, 16)
            act.wait_ge(const_t, 1)
            act.wait_ge(const_in, 16 * N_CONST)
            act.activation(wT_hi[:, :], ps_m[:, 0, 0:3 * H], ACT.Copy).then_inc(const_hi, 1)
            act.activation(brow_hi[:, :], brow[:, :], ACT.Copy).then_inc(const_hi, 1)

            def x_high(b):
                for k in range(2):
                    act.wait_ge(xt_tr, 2 * b + k + 1)
                    wait(act, u_ready, NB * b)
                    wait(act, h_ready, NB * b)
                    act.activation(xT_hi[:, k * HALF:(k + 1) * HALF], ps_m[:, k, :], ACT.Copy)\
                       .then_inc(xt_hi, 1)

            def exps(b, i):
                g = NB * b + i
                act.wait_ge(nbias_ready, g + 1)
                wait(act, d_ready, g - 1)
                act.activation(e_rows[:, i % 2, :], ps_u[:, :], ACT.Exp, bias=nbias[:, i % 2:i % 2 + 1],
                               scale=SCALE, accum_out=zsum[:, i:i + 1]).then_inc(exp_done, 1)

            def d_high(b, i):
                g = NB * b + i
                half, ii = i // HB, i % HB
                wait(act, ctx_done, 2 * b + half)
                for k in range(2):
                    act.wait_ge(dt_tr, 2 * g + k + 1)
                    src = ps_d[:, k, :].rearrange("p (j c) -> p j c", c=P)
                    if k == half:
                        act.activation(dT_hi[:, HB * k + ii:HB * k + HB, ii * P:(ii + 1) * P],
                                       src[:, ii:HB, :], ACT.Copy)
                        last = act.activation(dT_hi[:, HB * k:HB * k + ii + 1, (ii + 1) * P:(ii + 2) * P],
                                              src[:, 0:ii + 1, :], ACT.Copy)
                    else:
                        last = act.activation(dT_hi[:, HB * k:HB * k + HB, ii * P:(ii + 1) * P],
                                              src, ACT.Copy)
                    last.then_inc(dt_hi, 1)

            def a_out(b, i):
                g = NB * b + i
                if i == 0:
                    wait(act, y_done, 2 * b)
                for k in range(2):
                    act.wait_ge(at_tr, 2 * g + k + 1)
                    act.activation(aT[:, HB * k:HB * k + HB, i * P:(i + 1) * P],
                                   ps_m[:, k, :].rearrange("p (j c) -> p j c", c=P), ACT.Copy)\
                       .then_inc(at_done, 1)

            def degree(b, i):
                wait(act, deg_done, NB * b + i)
                act.wait_ge(a_in[i], 16 * (b + 1))
                act.activation(junk_a[:, :], a_rows[:, i, :], ACT.Copy, accum_out=deg[:, i:i + 1])\
                   .then_inc(deg_done, 1)

            def h_parts(b):
                wait(act, ctx_done, 2 * b)
                wait(act, self_done, 2 * b)
                for j in range(NB):
                    act.wait_ge(h_ready, NB * b + j + 1)
                    act.activation(h_hi[:, j, :], ps_m[:, (j + 1) % 2, 0:2 * H], ACT.Copy)\
                       .then_inc(h_high, 1)
                    act.activation(h_self[:, j, :], ps_m[:, (j + 1) % 2, 2 * H:3 * H], ACT.Copy)\
                       .then_inc(hs_ready, 1)

            def ctx_out(b, half):
                act.wait_ge(ctx_done, 2 * b + half + 1)
                wait(act, back_ready, 2 * b + half)
                act.activation(ctxT[:, :], ps_acc[:, half, :], ACT.Copy).then_inc(ctxT_ready, 1)

            def y_out(b, half):
                act.wait_ge(y_done, 2 * b + half + 1)
                act.activation(yT[:, half, :], ps_acc[:, half, :], ACT.Copy).then_inc(yT_ready, 1)

            def normalize(out_, in_, norm, half):
                for k in range(HB):
                    last = act.activation(out_[:, k, :], in_[:, k, :], ACT.Identity,
                                          bias=shift[norm][:, half, k:k + 1],
                                          scale=row_scales[norm][:, half, k:k + 1])
                return last

            def norm_c(b, half):
                act.wait_ge(c_scale, 2 * b + half + 1)
                c = c_rows[:, half, :, :]
                normalize(c, c, "c", half).then_inc(c_norm, 1)

            def norm_x(b, half):
                act.wait_ge(x_scale, 2 * b + half + 1)
                normalize(x1[:, HB * half:HB * (half + 1), :], c_rows[:, half, :, :], "x", half)\
                    .then_inc(x1_ready, 1)

            def norm_f(b, half):
                act.wait_ge(f_scale, 2 * b + half + 1)
                v = fin[:, half, :, :]
                normalize(v, v, "f", half).then_inc(f_norm, 1)
                act.wait_ge(f_norm, 2 * b + half + 1)
                act.dma_start(batch_rows(out, b, half * HALF, (half + 1) * HALF), v)\
                   .then_inc(out_done[half], 16)

            def batch(b, prev):
                p = b - 1
                x_high(b)
                if prev:
                    d_high(p, 7)
                    a_out(p, 6)
                exps(b, 0)
                if prev:
                    a_out(p, 7)
                    ctx_out(p, 1)
                    norm_x(p, 0)
                exps(b, 1)
                d_high(b, 0)
                degree(b, 0)
                h_parts(b)
                if prev:
                    norm_c(p, 1)
                exps(b, 2)
                d_high(b, 1)
                degree(b, 1)
                exps(b, 3)
                if prev:
                    norm_x(p, 1)
                d_high(b, 2)
                if prev:
                    y_out(p, 0)
                degree(b, 2)
                exps(b, 4)
                d_high(b, 3)
                degree(b, 3)
                if prev:
                    y_out(p, 1)
                a_out(b, 0)
                a_out(b, 1)
                ctx_out(b, 0)
                exps(b, 5)
                d_high(b, 4)
                degree(b, 4)
                exps(b, 6)
                d_high(b, 5)
                degree(b, 5)
                a_out(b, 2)
                exps(b, 7)
                if prev:
                    norm_f(p, 0)
                    norm_f(p, 1)
                d_high(b, 6)
                degree(b, 6)
                a_out(b, 3)
                norm_c(b, 0)
                a_out(b, 4)
                degree(b, 7)
                a_out(b, 5)

            batch(0, False)
            with act.Fori(1, B) as b:
                batch(b, True)
            e = B - 1
            d_high(e, 7)
            a_out(e, 6)
            a_out(e, 7)
            ctx_out(e, 1)
            norm_x(e, 0)
            norm_c(e, 1)
            norm_x(e, 1)
            y_out(e, 0)
            y_out(e, 1)
            norm_f(e, 0)
            norm_f(e, 1)
            for half in range(2):
                act.wait_ge(out_done[half], 16 * B)

        @block.vector
        def _(dve):
            def f(t):
                return t.bitcast(F32)

            dve.wait_ge(const_hi, 2)
            dve.tensor_tensor(wT_lo[:, :], ps_m[:, 0, 0:3 * H], f(wT_hi[:, :]), ALU.subtract)
            dve.wait_ge(const_gp, 9)
            dve.tensor_copy(bias2[0:1, :], f(brow_hi[0:1, :]))
            dve.tensor_tensor(bias2[32:33, :], brow[32:33, :], f(brow_hi[32:33, :]), ALU.subtract)
            dve.tensor_copy(ones[:, :], onesf[:, :]).then_inc(const_ok, 1)

            def x_low(b):
                for k in range(2):
                    dve.wait_ge(xt_hi, 2 * b + k + 1)
                    c = slice(k * HALF, (k + 1) * HALF)
                    dve.tensor_tensor(xT_lo[:, c], ps_m[:, k, :], f(xT_hi[:, c]), ALU.subtract)\
                       .then_inc(xt_split, 1)

            def row_max(b, i):
                g = NB * b + i
                s = slice(i % 2, i % 2 + 1)
                dve.wait_ge(u_ready, g + 1)
                dve.tensor_reduce(nmax[:, s], ps_u[:, :], AX.X, ALU.max, negate=True).then_inc(nmax_ready, 1)
                dve.wait_ge(nmax_ready, g + 1)
                dve.tensor_scalar(nbias[:, s], nmax[:, s], SCALE, None, ALU.mult).then_inc(nbias_ready, 1)

            def masked(b, i):
                g = NB * b + i
                dve.wait_ge(exp_done, g + 1)
                dve.wait_ge(a_in[i], 16 * (b + 1))
                wait(dve, dt_tr, 2 * (g - 1))
                dve.tensor_tensor_reduce(out=d_rows[:, i % 2, :], in0=e_rows[:, i % 2, :],
                                         in1=a_rows[:, i, :], scale=1.0, scalar=0.0, op0=ALU.mult,
                                         op1=ALU.add, accum_out=dsum[:, i:i + 1]).then_inc(d_ready, 1)

            def finish_d(b, i):
                g = NB * b + i
                half, ii = i // HB, i % HB
                dve.wait_ge(d_ready, g + 1)
                dve.wait_ge(diag_done, g) if not (isinstance(g, int) and g == 0) else None
                dve.tensor_tensor_reduce(out=junk[:, :], in0=d_rows[:, i % 2, i * P:(i + 1) * P],
                                         in1=ident[:, :], scale=1.0, scalar=0.0, op0=ALU.mult,
                                         op1=ALU.add, accum_out=ddiag[:, i:i + 1]).then_inc(diag_done, 1)
                for k in range(2):
                    dve.wait_ge(dt_hi, 2 * g + k + 1)
                    src = ps_d[:, k, :].rearrange("p (j c) -> p j c", c=P)
                    if k == half:
                        a = (slice(None), slice(HB * k + ii, HB * k + HB), slice(ii * P, (ii + 1) * P))
                        c = (slice(None), slice(HB * k, HB * k + ii + 1), slice((ii + 1) * P, (ii + 2) * P))
                        dve.tensor_tensor(dT_lo[a], src[:, ii:HB, :], f(dT_hi[a]), ALU.subtract)
                        last = dve.tensor_tensor(dT_lo[c], src[:, 0:ii + 1, :], f(dT_hi[c]), ALU.subtract)
                    else:
                        a = (slice(None), slice(HB * k, HB * k + HB), slice(ii * P, (ii + 1) * P))
                        last = dve.tensor_tensor(dT_lo[a], src, f(dT_hi[a]), ALU.subtract)
                    last.then_inc(dt_split, 1)
            def h_low(b):
                for j in range(NB):
                    dve.wait_ge(h_high, NB * b + j + 1)
                    dve.wait_ge(hs_ready, NB * b + j + 1)
                    dve.tensor_tensor(h_lo[:, j, :], ps_m[:, (j + 1) % 2, 0:2 * H], f(h_hi[:, j, :]),
                                      ALU.subtract).then_inc(h_split, 1)

            def add_self(b, half):
                n = 2 * b + half
                dve.wait_ge(back_ready, n + 1)
                dve.wait_ge(self_done, n + 1)
                c = c_rows[:, half, :, :]
                dve.tensor_tensor(c, ps_m[:, 0, :].rearrange("p (k h) -> p k h", h=H), c, ALU.add)\
                   .then_inc(back_read, 1)

            def stats_c(b, half):
                n = 2 * b + half
                cols = slice(HB * half, HB * (half + 1))
                base = 3 * n
                dve.scalar_tensor_tensor(out=rn2[:, half, :], in0=zsum[:, cols], scalar=EPS_RENORM,
                                         in1=dsum[:, cols], op0=ALU.mult, op1=ALU.add).then_inc(c_step, 1)
                dve.wait_ge(back_read, n + 1)
                for k in range(HB):
                    last = dve.bn_stats(stats["c"][:, half, k, :], c_rows[:, half, k, :])
                last.then_inc(c_step, 1)
                dve.wait_ge(c_step, base + 2)
                dve.reciprocal(rn[:, half, :], rn2[:, half, :]).then_inc(c_step, 1)
                for k in range(HB):
                    last = dve.bn_aggr(mv["c"][:, half, k, :], stats["c"][:, half, k, :])
                last.then_inc(c_small, 1)
                dve.wait_ge(c_step, base + 3)
                dve.tensor_tensor(rn2[:, half, :], rn[:, half, :], rn[:, half, :], ALU.mult)\
                   .then_inc(c_small, 1)
                dve.wait_ge(c_small, 3 * n + 2)
                dve.tensor_tensor(var["c"][:, half, :], mv["c"][:, half, :, 1], rn2[:, half, :], ALU.mult)\
                   .then_inc(c_small, 1)
                dve.tensor_scalar(nmean["c"][:, half, :], mv["c"][:, half, :, 0], -1.0, None, ALU.mult)\
                   .then_inc(c_var, 1)
                dve.wait_ge(c_small, 3 * n + 3)
                dve.tensor_scalar(var["c"][:, half, :], var["c"][:, half, :], EPS_CTX, None, ALU.add)\
                   .then_inc(c_var, 1)

            def stats_x(b, half):
                n = 2 * b + half
                cols = slice(HB * half, HB * (half + 1))
                base = 3 * n
                dve.wait_ge(affine_b, n + 1)
                dve.wait_ge(xres_in, 16 * (b + 1))
                c = c_rows[:, half, :, :]
                dve.scalar_tensor_tensor(out=c, in0=c, scalar=0.0, in1=x_res[:, cols, :],
                                         op0=ALU.max, op1=ALU.add).then_inc(x_step, 1)
                dve.wait_ge(x_step, base + 1)
                for k in range(HB):
                    last = dve.bn_stats(stats["x"][:, half, k, :], c_rows[:, half, k, :])
                last.then_inc(x_step, 1)
                dve.wait_ge(deg_done, NB * b + HB * (half + 1))
                dve.tensor_scalar(vdeg[:, half, :], deg[:, cols], EPS_DEG, None, ALU.add).then_inc(x_var, 1)
                dve.wait_ge(x_step, base + 2)
                dve.sem_inc(x_step, 1)
                for k in range(HB):
                    last = dve.bn_aggr(mv["x"][:, half, k, :], stats["x"][:, half, k, :])
                last.then_inc(x_small, 1)
                dve.wait_ge(x_small, n + 1)
                dve.tensor_scalar(var["x"][:, half, :], mv["x"][:, half, :, 1], EPS_LN, None, ALU.add)\
                   .then_inc(x_var, 1)
                dve.tensor_scalar(nmean["x"][:, half, :], mv["x"][:, half, :, 0], -1.0, None, ALU.mult)\
                   .then_inc(x_var, 1)

            def add_out(b, half):
                n = 2 * b + half
                dve.wait_ge(o_ready, n + 1)
                dve.wait_ge(x1b_ready, n + 1)
                dve.wait_ge(dinv_ready, n + 1)
                for k in range(HB):
                    i = HB * half + k
                    last = dve.scalar_tensor_tensor(out=fin[:, half, k, :], in0=ps_m[:, half, k * P:(k + 1) * P],
                                                    scalar=dinv[:, i:i + 1], in1=x1b[:, i, :],
                                                    op0=ALU.mult, op1=ALU.add)
                last.then_inc(o_read, 1)

            def stats_f(b, half):
                n = 2 * b + half
                dve.wait_ge(o_read, n + 1)
                for k in range(HB):
                    last = dve.bn_stats(stats["f"][:, half, k, :], fin[:, half, k, :])
                last.then_inc(f_step, 1)
                dve.wait_ge(f_step, 2 * n + 1)
                dve.sem_inc(f_step, 1)
                for k in range(HB):
                    last = dve.bn_aggr(mv["f"][:, half, k, :], stats["f"][:, half, k, :])
                last.then_inc(f_small, 1)
                dve.wait_ge(f_small, n + 1)
                dve.tensor_scalar(var["f"][:, half, :], mv["f"][:, half, :, 1], EPS_LN, None, ALU.add)\
                   .then_inc(f_var, 1)
                dve.tensor_scalar(nmean["f"][:, half, :], mv["f"][:, half, :, 0], -1.0, None, ALU.mult)\
                   .then_inc(f_var, 1)

            def batch(b, prev):
                p = b - 1
                if prev:
                    masked(p, 7)
                x_low(b)
                if prev:
                    finish_d(p, 7)
                row_max(b, 0)
                if prev:
                    stats_x(p, 0)
                masked(b, 0)
                row_max(b, 1)
                if prev:
                    add_self(p, 1)
                    stats_c(p, 1)
                finish_d(b, 0)
                h_low(b)
                masked(b, 1)
                row_max(b, 2)
                finish_d(b, 1)
                if prev:
                    stats_x(p, 1)
                for i in (2, 3):
                    masked(b, i)
                    row_max(b, i + 1)
                    finish_d(b, i)
                masked(b, 4)
                row_max(b, 5)
                finish_d(b, 4)
                masked(b, 5)
                if prev:
                    add_out(p, 0)
                    add_out(p, 1)
                add_self(b, 0)
                row_max(b, 6)
                if prev:
                    stats_f(p, 0)
                    stats_f(p, 1)
                stats_c(b, 0)
                finish_d(b, 5)
                masked(b, 6)
                row_max(b, 7)
                finish_d(b, 6)
                for half in range(2):
                    wait(dve, out_done[half], 16 * b)

            batch(0, False)
            with dve.Fori(1, B) as b:
                batch(b, True)
            e = B - 1
            masked(e, 7)
            finish_d(e, 7)
            stats_x(e, 0)
            add_self(e, 1)
            stats_c(e, 1)
            stats_x(e, 1)
            add_out(e, 0)
            add_out(e, 1)
            stats_f(e, 0)
            stats_f(e, 1)

        @block.gpsimd
        def _(pool):
            pool.memset(brow[:, :], 0.0).then_inc(const_gp, 1)
            pool.memset(ident[:, :], 0.0).then_inc(const_gp, 1)
            pool.memset(onesf[:, :], 1.0).then_inc(const_gp, 1)
            pool.memset(bias2[:, :].bitcast(F32), 0.0).then_inc(const_gp, 1)
            pool.memset(sides[:, :], 1.0).then_inc(const_gp, 1)
            pool.memset(minus_half[:, :], -0.5).then_inc(const_gp, 1)
            pool.wait_ge(const_gp, 6)
            pool.affine_select(out=ident[:, :], in_=ident[:, :], compare_op=ALU.not_equal, fill=1.0,
                               base=0, pattern=[[-1, P]], channel_multiplier=1).then_inc(const_gp, 1)
            for k, sign in ((0, 1), (1, -1)):
                v = sides[:, k * P:(k + 1) * P]
                pool.affine_select(out=v, in_=v, compare_op=ALU.is_gt, fill=0.0, base=0,
                                   pattern=[[-sign, P]], channel_multiplier=sign).then_inc(const_gp, 1)
            pool.wait_ge(const_gp, 9)
            pool.wait_ge(bcast_in, 48)

            def bc(t):
                return t[:, :].rearrange("p (a h) -> p a h", a=1).to_broadcast([P, HB, H])

            def per_row(t):
                return t.rearrange("p (j a) -> p j a", a=1).to_broadcast([P, HB, H])

            def masks(b, i):
                g = NB * b + i
                half, ii = i // HB, i % HB
                pool.wait_ge(dt_split, 2 * g + half + 1)
                for t in (dT_hi, dT_lo):
                    v = t[:, i, ii * P:(ii + 2) * P]
                    pool.tensor_tensor(v, v.bitcast(F32), sides[:, :], ALU.mult).then_inc(mask_done, 1)

            def self_term(b, half):
                i = HB * half
                pool.wait_ge(diag_done, NB * b + HB * (half + 1))
                pool.wait_ge(hs_ready, NB * (b + 1))
                pool.tensor_tensor(c_rows[:, half, :, :], h_self[:, i:i + HB, :],
                                   per_row(ddiag[:, i:i + HB]), ALU.mult).then_inc(self_done, 1)

            def row_scale(norm, half, power_done, scaled, done, n, more=None):
                pool.tensor_tensor(power[norm][:, half, :], var[norm][:, half, :], minus_half[:, :], ALU.pow)\
                    .then_inc(power_done, 1)
                pool.wait_ge(power_done, n + 1)
                s = power[norm]
                if more is not None:
                    s = scale[norm]
                    pool.tensor_tensor(s[:, half, :], power[norm][:, half, :], more[:, half, :], ALU.mult)\
                        .then_inc(scaled, 1)
                    pool.wait_ge(scaled, n + 1)
                pool.tensor_tensor(shift[norm][:, half, :], s[:, half, :], nmean[norm][:, half, :], ALU.mult)\
                    .then_inc(done, 1)

            def scale_c(b, half):
                n = 2 * b + half
                pool.wait_ge(c_var, 2 * (n + 1))
                row_scale("c", half, c_power, c_scaled, c_scale, n, rn)

            def affine(b, half):
                n = 2 * b + half
                c = c_rows[:, half, :, :]
                pool.wait_ge(c_norm, n + 1)
                pool.tensor_tensor(c, c, bc(lnw_bc), ALU.mult).then_inc(affine_w, 1)
                pool.wait_ge(affine_w, n + 1)
                pool.tensor_tensor(c, c, bc(lnb_bc), ALU.add).then_inc(affine_b, 1)

            def scale_x(b, half):
                n = 2 * b + half
                pool.wait_ge(x_var, 3 * (n + 1))
                row_scale("x", half, x_power, None, x_scale, n)
                i = HB * half
                pool.tensor_tensor(dinv[:, i:i + HB], vdeg[:, half, :], minus_half[:, :], ALU.pow)\
                    .then_inc(dinv_ready, 1)

            def times_degree(b, half):
                n = 2 * b + half
                cols = slice(HB * half, HB * (half + 1))
                pool.wait_ge(x1_ready, n + 1)
                pool.wait_ge(dinv_ready, n + 1)
                pool.tensor_tensor(x1p[:, cols, :], x1[:, cols, :], per_row(dinv[:, cols]), ALU.mult)\
                    .then_inc(x1p_ready, 1)
                pool.tensor_tensor(x1b[:, cols, :], x1[:, cols, :], bc(b1_bc), ALU.add)\
                    .then_inc(x1b_ready, 1)

            def scale_f(b, half):
                n = 2 * b + half
                pool.wait_ge(f_var, 2 * (n + 1))
                row_scale("f", half, f_power, None, f_scale, n)

            def batch(b, prev):
                p = b - 1
                if prev:
                    masks(p, 7)
                    self_term(p, 1)
                    scale_x(p, 0)
                    times_degree(p, 0)
                    scale_c(p, 1)
                masks(b, 0)
                if prev:
                    affine(p, 1)
                masks(b, 1)
                if prev:
                    scale_x(p, 1)
                    times_degree(p, 1)
                masks(b, 2)
                masks(b, 3)
                self_term(b, 0)
                masks(b, 4)
                if prev:
                    scale_f(p, 0)
                    scale_f(p, 1)
                scale_c(b, 0)
                masks(b, 5)
                masks(b, 6)
                affine(b, 0)

            batch(0, False)
            with pool.Fori(1, B) as b:
                batch(b, True)
            e = B - 1
            masks(e, 7)
            self_term(e, 1)
            scale_x(e, 0)
            times_degree(e, 0)
            scale_c(e, 1)
            affine(e, 1)
            scale_x(e, 1)
            times_degree(e, 1)
            scale_f(e, 0)
            scale_f(e, 1)


_INS = ['x', 'adj', 'L0_gnn_Wl', 'L0_gnn_bl', 'L0_gnn_Ws', 'L0_gnn_bs', 'L0_gnn_Wr', 'L0_gnn_br',
        'L0_gnn_ln_w', 'L0_gnn_ln_b', 'L1_gnn_weight', 'L1_gnn_bias']


def kernel(**inputs):
    import numpy as _np
    import concourse.bacc as _bacc
    from concourse import mybir as _mybir
    from concourse.bass_utils import run_bass_kernel_spmd as _run

    nc = _bacc.Bacc("TRN2", target_bir_lowering=False, num_devices=1)
    arrays, args = {}, []
    for name in _INS:
        a = _np.ascontiguousarray(inputs[name])
        arrays[f"in_{name}_dram"] = a
        args.append(nc.dram_tensor(f"in_{name}_dram", a.shape, _mybir.dt.from_np(a.dtype), kind="ExternalInput").ap())
    shape = arrays["in_x_dram"].shape
    args.append(nc.dram_tensor("out_0_dram", shape, _mybir.dt.float32, kind="ExternalOutput").ap())
    two_layer_graph_kernel(nc, *args)
    r = _run(nc, [arrays], core_ids=[0])
    return r.results[0]["out_0_dram"]
```

```python
from contextlib import ExitStack

import concourse.bass as bass
from concourse import mybir

F32 = mybir.dt.float32
F32R = mybir.dt.float32r
ALU = mybir.AluOpType
ACT = mybir.ActivationFunctionType
AX = mybir.AxisListType

P = 128
EPS_RENORM = 1e-10
EPS_CTX = 1e-12
EPS_LN = 1e-5
EPS_DEG = 1e-5


def wait(eng, sem, value):
    if isinstance(value, int) and value <= 0:
        return
    eng.wait_ge(sem, value)


def two_layer_graph_kernel(nc, x, adj, Wl, bl, Ws, bs, Wr, br, ln_w, ln_b, W1, b1, out):
    B, N, H = x.shape
    NB = N // P
    HB = NB // 2
    HALF = N // 2
    QUART = N // 4
    SCALE = float(H) ** -0.5
    assert H == P and NB == 8 and HALF == 512

    with ExitStack() as ctx:
        def sb(name, shape, dt=F32):
            return ctx.enter_context(nc.sbuf_tensor(name, shape, dt))

        def pb(name, shape):
            return ctx.enter_context(nc.psum_tensor(name, shape, F32))

        def sem(name):
            return ctx.enter_context(nc.semaphore(name))

        ident = sb("ident", [P, P])
        sides = sb("sides", [P, 2 * P])
        wraw = sb("wraw", [P, 3, H])
        wT_hi = sb("wT_hi", [P, 3 * H], F32R)
        wT_lo = sb("wT_lo", [P, 3 * H], F32R)
        bias_bc = sb("bias_bc", [P, 3 * H])
        w1_sb = sb("w1_sb", [P, H])
        lnw_bc = sb("lnw_bc", [P, H])
        lnb_bc = sb("lnb_bc", [P, H])
        b1_bc = sb("b1_bc", [P, H])

        x_rows = sb("x_rows", [P, NB, H])
        x_res = sb("x_res", [P, NB, H])
        xT_hi = sb("xT_hi", [P, N], F32R)
        xT_lo = sb("xT_lo", [P, N], F32R)
        h_hi = sb("h_hi", [P, NB, 2 * H], F32R)
        h_lo = sb("h_lo", [P, NB, 2 * H], F32R)
        h_sum = sb("h_sum", [P, NB, 3 * H])
        a_rows = sb("a_rows", [P, NB, N])
        aT = sb("aT", [P, NB, N])
        e_rows = sb("e_rows", [P, 2, N])
        d_rows = sb("d_rows", [P, 2, N])
        dT_hi = sb("dT_hi", [P, 2, NB, QUART + P], F32R)
        dT_lo = sb("dT_lo", [P, 2, NB, QUART + P], F32R)
        ctxT = sb("ctxT", [P, HALF])
        yT = sb("yT", [P, 2, HALF])
        c_rows = sb("c_rows", [P, 2, HB, H])
        x1p = sb("x1p", [P, NB, H])
        x1b = sb("x1b", [P, NB, H])
        fin = sb("fin", [P, 2, HB, H])
        junk = sb("junk", [P, P])
        junk_a = sb("junk_a", [P, N], mybir.dt.bfloat16)
        nmax = sb("nmax", [P, 2])
        nbias = sb("nbias", [P, 2])
        zsum = sb("zsum", [P, NB])
        dsum = sb("dsum", [P, NB])
        ddiag = sb("ddiag", [P, NB])
        deg = sb("deg", [P, NB])
        dinv = sb("dinv", [P, NB])
        minus_half = sb("minus_half", [P, HB])
        rn = sb("rn", [P, 2, HB])
        rn2 = sb("rn2", [P, 2, HB])
        vdeg = sb("vdeg", [P, 2, HB])
        NORMS = ("c", "x", "f")
        stats = {k: sb(f"stats_{k}", [P, 2, HB, 6]) for k in NORMS}
        mv = {k: sb(f"mv_{k}", [P, 2, HB, 2]) for k in NORMS}
        nmean = {k: sb(f"nmean_{k}", [P, 2, HB]) for k in NORMS}
        var = {k: sb(f"var_{k}", [P, 2, HB]) for k in NORMS}
        power = {k: sb(f"power_{k}", [P, 2, HB]) for k in NORMS}
        scale = {k: sb(f"scale_{k}", [P, 2, HB]) for k in NORMS}
        shift = {k: sb(f"shift_{k}", [P, 2, HB]) for k in NORMS}

        row_scales = {"c": scale["c"], "x": power["x"], "f": power["f"]}

        ps_u = pb("ps_u", [P, N])
        ps_d = pb("ps_d", [P, 2, HALF])
        ps_m = pb("ps_m", [P, 2, HALF])
        ps_ctx = pb("ps_ctx", [P, 2, QUART])
        ps_y = pb("ps_y", [P, HALF])


        const_in = sem("const_in")
        bias_in = sem("bias_in")
        const_gp = sem("const_gp")
        const_t = sem("const_t")
        bcast_in = sem("bcast_in")
        const_hi = sem("const_hi")
        const_ok = sem("const_ok")
        x_in = sem("x_in")
        xres_in = sem("xres_in")
        a_in = [sem(f"a_in{i}") for i in range(NB)]
        xt_tr = sem("xt_tr")
        xt_hi = sem("xt_hi")
        xt_split = sem("xt_split")
        u_ready = sem("u_ready")
        nmax_ready = sem("nmax_ready")
        nbias_ready = sem("nbias_ready")
        exp_done = sem("exp_done")
        d_ready = sem("d_ready")
        diag_done = sem("diag_done")
        dt_tr = sem("dt_tr")
        dt_hi = sem("dt_hi")
        dt_split = sem("dt_split")
        mask_done = sem("mask_done")
        at_tr = sem("at_tr")
        at_done = sem("at_done")
        h_ready = sem("h_ready")
        h_added = sem("h_added")
        h_high = sem("h_high")
        h_split = sem("h_split")
        deg_done = sem("deg_done")
        ctx_done = sem("ctx_done")
        ctxT_ready = sem("ctxT_ready")
        self_done = sem("self_done")
        back_ready = sem("back_ready")
        back_read = sem("back_read")
        c_step = sem("c_step")
        c_var = sem("c_var")
        c_power = sem("c_power")
        c_scaled = sem("c_scaled")
        x_power = sem("x_power")
        f_power = sem("f_power")
        c_small = sem("c_small")
        c_scale = sem("c_scale")
        c_norm = sem("c_norm")
        affine_w = sem("affine_w")
        affine_b = sem("affine_b")
        x_step = sem("x_step")
        x_var = sem("x_var")
        x_small = sem("x_small")
        x_scale = sem("x_scale")
        dinv_ready = sem("dinv_ready")
        x1_ready = sem("x1_ready")
        x1p_ready = sem("x1p_ready")
        x1b_ready = sem("x1b_ready")
        y_done = sem("y_done")
        yT_ready = sem("yT_ready")
        o_ready = sem("o_ready")
        o_read = sem("o_read")
        f_step = sem("f_step")
        f_var = sem("f_var")
        f_small = sem("f_small")
        f_scale = sem("f_scale")
        f_norm = sem("f_norm")
        last_norm = sem("last_norm")
        last_stored = sem("last_stored")
        fin_free = [sem(f"fin_free{h}") for h in range(2)]

        def batch_rows(t, b, r0, r1):
            v = t[bass.ds(b, 1), r0:r1, :]
            return v.rearrange("o (j p) h -> p (o j) h", p=P)

        def block_rows(t, b, i):
            return t[bass.ds(b, 1), i * P:(i + 1) * P, :].rearrange("o p m -> (o p) m")

        def h_bank(j):
            if j in (4, 7):
                return ps_ctx[:, :, :].rearrange("p a c -> p (a c)")
            return ps_m[:, (j if j < 4 else j - 1) % 2, :]


        def y_bank(b, half):
            return ps_u[:, HALF:N] if half and isinstance(b, int) else ps_y[:, :]

        def o_bank(b, half):
            return ps_m[:, 0 if half and isinstance(b, int) else 1, :]

        X_TURN = 10

        def adj_turn(i, k):
            return 2 * i + k + (2 if i >= X_TURN // 2 else 0)

        def turn_bank(t):
            return (ps_m[:, 0, :], ps_y[:, :], ps_m[:, 1, :])[t % 3]

        def bc(t):
            return t[:, :].rearrange("p (a h) -> p a h", a=1).to_broadcast([P, HB, H])

        def affine_on(eng, b, half):
            n = 2 * b + half
            c = c_rows[:, half, :, :]
            eng.wait_ge(c_norm, n + 1)
            eng.tensor_tensor(c, c, bc(lnw_bc), ALU.mult).then_inc(affine_w, 1)
            eng.wait_ge(affine_w, n + 1)
            eng.tensor_tensor(c, c, bc(lnb_bc), ALU.add).then_inc(affine_b, 1)

        block = ctx.enter_context(nc.Block())

        @block.sync
        def _(sp):
            def load_a(b, i):
                g = NB * b + i
                wait(sp, at_tr, 2 * (g - NB + 1))
                sp.dma_start(a_rows[:, i, :], block_rows(adj, b, i)).then_inc(a_in[i], 16)

            def load_x(b):
                wait(sp, xt_tr, 2 * b)
                sp.dma_start(x_rows[:, :, :], batch_rows(x, b, 0, N)).then_inc(x_in, 16)

            def load_xres(b):
                wait(sp, x_step, 3 * 2 * b)
                sp.dma_start(x_res[:, :, :], batch_rows(x, b, 0, N)).then_inc(xres_in, 16)

            load_x(0)
            load_a(0, 0)
            for k, w in enumerate((Wl, Wr, Ws)):
                sp.dma_start(wraw[:, k, :], w).then_inc(const_in, 16)
            load_a(0, 1)
            for k, v in enumerate((bl, br, bs)):
                sp.dma_start(bias_bc[:, k * H:(k + 1) * H], v.partition_broadcast(P)).then_inc(bias_in, 16)
            load_a(0, 2)
            for t, v in ((lnw_bc, ln_w), (lnb_bc, ln_b), (b1_bc, b1)):
                sp.dma_start(t[:, :], v.partition_broadcast(P)).then_inc(bcast_in, 16)
            for i in range(3, NB):
                load_a(0, i)
            load_xres(0)
            with sp.Fori(1, B) as b:
                load_x(b)
                for i in range(NB):
                    if i == 4:
                        load_xres(b)
                    load_a(b, i)

        @block.tensor
        def _(pe):
            def split_matmul(o, hi_l, lo_l, hi_r, lo_r, start, stop):
                pe.matmul(o, hi_l, hi_r, start=start, stop=False)
                pe.matmul(o, hi_l, lo_r, start=False, stop=False)
                return pe.matmul(o, lo_l, hi_r, start=False, stop=stop)


            def turn_read(b, t):
                if X_TURN <= t < X_TURN + 2:
                    pe.wait_ge(xt_split, 2 * (b + 1) + t - X_TURN + 1)
                else:
                    pe.wait_ge(at_done, 2 * NB * b + (t if t < X_TURN else t - 2) + 1)

            def turn_x(b, k):
                pe.wait_ge(x_in, 16 * (b + 1))
                t = X_TURN + k
                if not isinstance(b, int):
                    turn_read(b - 1, t - 3)
                for j in range(HB):
                    last = pe.transpose(turn_bank(t)[:, j * P:(j + 1) * P],
                                        x_rows[:, HB * k + j, :], ident[:, :])
                last.then_inc(xt_tr, 1)

            def scores(b, i):
                g = NB * b + i
                pe.wait_ge(xt_split, 2 * (b + 1))
                wait(pe, exp_done, g)
                s = slice(i * P, (i + 1) * P)
                for k in range(2):
                    c = slice(k * HALF, (k + 1) * HALF)
                    last = split_matmul(ps_u[:, c], xT_hi[:, s], xT_lo[:, s],
                                        xT_hi[:, c], xT_lo[:, c], True, True)
                last.then_inc(u_ready, 1)

            def project(b, j):
                if j == 0:
                    pe.wait_ge(xt_split, 2 * (b + 1))
                if j < 2 and not isinstance(b, int):
                    pe.wait_ge(at_done, 2 * NB * b)
                elif j == 0:
                    pe.wait_ge(const_ok, 1)
                elif j == 4 and not isinstance(b, int):
                    pe.wait_ge(back_read, 2 * b)
                before = {2: 0, 3: 1, 5: 2, 6: 3, 7: 4}
                if j in before:
                    pe.wait_ge(h_added, NB * b + before[j] + 1)
                o = h_bank(j)[:, 0:3 * H]
                s = slice(j * P, (j + 1) * P)
                split_matmul(o, xT_hi[:, s], xT_lo[:, s], wT_hi[:, :], wT_lo[:, :],
                             True, True).then_inc(h_ready, 1)

            def turn_d(b, i):
                g = NB * b + i
                pe.wait_ge(d_ready, g + 1)
                wait(pe, dt_split, g)
                for k in range(2):
                    for j in range(HB):
                        c = (HB * k + j) * P
                        last = pe.transpose(ps_d[:, k, j * P:(j + 1) * P],
                                            d_rows[:, i % 2, c:c + P], ident[:, :])
                last.then_inc(dt_tr, 1)

            def turn_a(b, i, k):
                g, t = NB * b + i, adj_turn(i, k)
                first = isinstance(b, int) and b == 0
                last = isinstance(b, int) and b == B - 1
                pe.wait_ge(a_in[i], 16 * (b + 1))
                pe.wait_ge(d_ready, g + 1)
                pe.wait_ge(deg_done, g + 1)
                if t >= 3:
                    before = t - 3
                    if last and X_TURN <= before < X_TURN + 2:
                        before -= 3
                    turn_read(b, before)
                elif t == 0:
                    pe.wait_ge(h_added, NB * (b + 1))
                elif t == 1 and not first:
                    pe.wait_ge(yT_ready, 2 * b)
                elif t == 2 and first:
                    pe.wait_ge(h_added, NB * (b + 1))
                elif t == 2:
                    pe.wait_ge(o_read, 2 * b)
                elif first:
                    pe.wait_ge(xt_split, 2 * (b + 1))
                for j in range(HB):
                    c = (HB * k + j) * P
                    end = pe.transpose(turn_bank(t)[:, j * P:(j + 1) * P],
                                       a_rows[:, i, c:c + P], ident[:, :])
                end.then_inc(at_tr, 1)

            def context(b, q, t0=0, t1=NB):
                g = NB * b + 2 * q
                if t0 == 0:
                    pe.wait_ge(dt_split, g + 2)
                    pe.wait_ge(mask_done, 4 * (g + 2))
                    pe.wait_ge(h_split, HB * (b + 1))
                    wait(pe, ctxT_ready, 4 * b + q)
                    if q == 2:
                        pe.wait_ge(back_read, 2 * b + 1)
                acc, slot = ps_ctx[:, q % 2, :], q % 2
                L, R = slice(0, H), slice(H, 2 * H)
                near = (2 * q, 2 * q + 1)
                whole, copy = slice(0, QUART), slice(QUART, QUART + P)
                order = [j for j in range(NB) if j not in near] + list(near)

                def part(o, j, side, cols, start=False, stop=False):
                    return split_matmul(o, h_hi[:, j, side], h_lo[:, j, side], dT_hi[:, slot, j, cols],
                                        dT_lo[:, slot, j, cols], start, stop)

                for t in range(t0, t1):
                    j = order[t]
                    if j == near[0]:
                        part(acc[:, 0:P], j, L, copy)
                        part(acc, j, R, whole)
                    elif j == near[1]:
                        part(acc[:, P:QUART], j, R, copy)
                        part(acc, j, L, whole, stop=True).then_inc(ctx_done, 1)
                    else:
                        part(acc, j, L if j > near[1] else R, whole, start=t == 0)

            def turn_back(b, half):
                pe.wait_ge(ctxT_ready, 4 * b + 2 * half + 2)
                for j in range(HB):
                    last = pe.transpose(ps_ctx[:, j // 2, (j % 2) * P:(j % 2 + 1) * P],
                                        ctxT[:, j * P:(j + 1) * P], ident[:, :])
                last.then_inc(back_ready, 1)

            def gather(b, half, j0, j1):
                pe.wait_ge(at_done, 2 * NB * (b + 1))
                pe.wait_ge(x1p_ready, 2 * b + (j1 - 1) // HB + 1)
                if j0 == 0 and half == 1:
                    if isinstance(b, int):
                        pe.wait_ge(exp_done, NB * B)
                    else:
                        pe.wait_ge(yT_ready, 2 * b + 1)
                for j in range(j0, j1):
                    last = pe.matmul(y_bank(b, half), x1p[:, j, :],
                                     aT[:, j, half * HALF:(half + 1) * HALF],
                                     start=j == 0, stop=j == NB - 1)
                if j1 == NB:
                    last.then_inc(y_done, 1)

            def second_product(b, half):
                pe.wait_ge(yT_ready, 2 * b + half + 1)
                if isinstance(b, int):
                    pe.wait_ge(at_done, 2 * NB * (b + 1))
                elif half:
                    pe.wait_ge(o_read, 2 * b + 1)
                else:
                    pe.wait_ge(h_added, NB * (b + 2))
                for j in range(HB):
                    last = pe.matmul(o_bank(b, half)[:, j * P:(j + 1) * P], yT[:, half, j * P:(j + 1) * P],
                                     w1_sb[:, :], start=True, stop=True)
                last.then_inc(o_ready, 1)

            def weights():
                pe.wait_ge(const_in, 16 * 3)
                for half in range(2):
                    pe.wait_ge(fin_free[half], 16)
                for k in range(3):
                    last = pe.transpose(ps_m[:, 0, k * H:(k + 1) * H], wraw[:, k, :], ident[:, :])
                last.then_inc(const_t, 1)

            def first_batch(b):
                turn_x(b, 0)
                turn_x(b, 1)
                weights()
                scores(b, 0)
                project(b, 0)
                project(b, 1)
                project(b, 2)
                scores(b, 1)
                turn_d(b, 0)
                project(b, 3)
                project(b, 4)
                project(b, 5)
                project(b, 6)
                scores(b, 2)
                turn_d(b, 1)
                project(b, 7)
                scores(b, 3)
                turn_a(b, 0, 0)
                turn_a(b, 0, 1)
                turn_a(b, 1, 0)
                scores(b, 4)
                turn_d(b, 2)
                context(b, 0, 0, 3)
                turn_a(b, 1, 1)
                context(b, 0, 3, 4)
                turn_a(b, 2, 0)
                context(b, 0, 4, 5)
                scores(b, 5)
                turn_d(b, 3)
                context(b, 0, 5, 8)
                turn_a(b, 2, 1)
                scores(b, 6)
                turn_d(b, 4)
                context(b, 1, 0, 8)
                turn_back(b, 0)
                scores(b, 7)
                turn_d(b, 5)
                turn_d(b, 6)
                turn_a(b, 3, 0)
                context(b, 2, 0, 1)
                turn_a(b, 3, 1)
                context(b, 2, 1, 2)
                turn_a(b, 4, 0)
                turn_a(b, 4, 1)
                context(b, 2, 2, 4)

            def batch(b, p):
                turn_x(b, 0)
                context(p, 2, 4, 5)
                turn_x(b, 1)
                turn_a(p, 5, 0)
                turn_d(p, 7)
                turn_a(p, 5, 1)
                scores(b, 0)
                context(p, 2, 5, 6)
                turn_a(p, 6, 0)
                turn_a(p, 6, 1)
                turn_a(p, 7, 0)
                context(p, 2, 6, 8)
                turn_a(p, 7, 1)
                scores(b, 1)
                turn_d(b, 0)
                project(b, 0)
                context(p, 3, 0, 6)
                scores(b, 2)
                context(p, 3, 6, 8)
                project(b, 1)
                project(b, 2)
                turn_back(p, 1)
                project(b, 3)
                turn_d(b, 1)
                scores(b, 3)
                gather(p, 0, 0, 1)
                project(b, 4)
                project(b, 5)
                gather(p, 0, 1, 2)
                project(b, 6)
                scores(b, 4)
                project(b, 7)
                turn_d(b, 2)
                gather(p, 0, 2, 4)
                turn_a(b, 0, 0)
                scores(b, 5)
                context(b, 0, 0, 7)
                turn_d(b, 3)
                context(b, 0, 7, 8)
                gather(p, 0, 4, 8)
                scores(b, 6)
                context(b, 1, 0, 1)
                second_product(p, 0)
                context(b, 1, 1, 4)
                turn_d(b, 4)
                context(b, 1, 4, 8)
                scores(b, 7)
                turn_back(b, 0)
                gather(p, 1, 0, 2)
                turn_d(b, 5)
                gather(p, 1, 2, 8)
                turn_d(b, 6)
                second_product(p, 1)
                context(b, 2, 0, 1)
                turn_a(b, 0, 1)
                context(b, 2, 1, 3)
                turn_a(b, 1, 0)
                turn_a(b, 1, 1)
                turn_a(b, 2, 0)
                turn_a(b, 2, 1)
                context(b, 2, 3, 4)
                turn_a(b, 3, 0)
                turn_a(b, 3, 1)
                turn_a(b, 4, 0)
                turn_a(b, 4, 1)

            def last_batch(p):
                turn_d(p, 7)
                context(p, 2, 4, 5)
                turn_a(p, 5, 0)
                turn_a(p, 5, 1)
                context(p, 2, 5, 6)
                turn_a(p, 6, 0)
                turn_a(p, 6, 1)
                context(p, 2, 6, 7)
                turn_a(p, 7, 0)
                context(p, 2, 7, 8)
                turn_a(p, 7, 1)
                context(p, 3, 0, 8)
                turn_back(p, 1)
                gather(p, 1, 0, 1)
                gather(p, 0, 0, 2)
                gather(p, 1, 1, 2)
                gather(p, 0, 2, 3)
                gather(p, 1, 2, 3)
                gather(p, 0, 3, 4)
                gather(p, 1, 3, 4)
                gather(p, 0, 4, 8)
                gather(p, 1, 4, 6)
                second_product(p, 0)
                gather(p, 1, 6, 8)
                second_product(p, 1)

            pe.wait_ge(const_gp, 6)
            first_batch(0)
            with pe.Fori(1, B) as b:
                batch(b, b - 1)
            last_batch(B - 1)

        @block.scalar
        def _(act):

            def weights():
                act.wait_ge(const_t, 1)
                act.activation(wT_hi[:, :], ps_m[:, 0, 0:3 * H], ACT.Copy).then_inc(const_hi, 1)

            def x_high(b, k):
                act.wait_ge(xt_tr, 2 * b + k + 1)
                wait(act, u_ready, NB * b)
                wait(act, h_ready, NB * b)
                act.activation(xT_hi[:, k * HALF:(k + 1) * HALF], turn_bank(X_TURN + k), ACT.Copy)\
                   .then_inc(xt_hi, 1)

            def exps(b, i):
                g = NB * b + i
                act.wait_ge(nbias_ready, g + 1)
                wait(act, d_ready, g - 1)
                wait(act, c_step, 6 * b + 3 * (i // HB) - 5)
                act.activation(e_rows[:, i % 2, :], ps_u[:, :], ACT.Exp, bias=nbias[:, i % 2:i % 2 + 1],
                               scale=SCALE, accum_out=zsum[:, i:i + 1]).then_inc(exp_done, 1)

            def d_high(b, i):
                g, q, c = NB * b + i, i // 2, (i % 2) * P
                wait(act, ctx_done, 4 * b + q - 1)
                act.wait_ge(dt_tr, g + 1)
                act.activation(dT_hi[:, q % 2, :, c:c + P],
                               ps_d[:, :, :].rearrange("p k (j c) -> p (k j) c", c=P), ACT.Copy)\
                   .then_inc(dt_hi, 1)

            def a_out(b, i, k):
                g = NB * b + i
                if i == 0 and k == 0:
                    wait(act, y_done, 2 * b)
                act.wait_ge(at_tr, 2 * g + k + 1)
                act.activation(aT[:, HB * k:HB * k + HB, i * P:(i + 1) * P],
                               turn_bank(adj_turn(i, k)).rearrange("p (j c) -> p j c", c=P), ACT.Copy)\
                   .then_inc(at_done, 1)

            def degree(b, i):
                wait(act, deg_done, NB * b + i)
                wait(act, x_var, 6 * b + 3 * (i // HB) - 5)
                act.wait_ge(a_in[i], 16 * (b + 1))
                act.activation(junk_a[:, :], a_rows[:, i, :], ACT.Copy, accum_out=deg[:, i:i + 1])\
                   .then_inc(deg_done, 1)

            def h_part(b, jj):
                if jj == 0:
                    wait(act, ctx_done, 4 * b)
                j = 2 * jj
                act.wait_ge(h_added, NB * b + j + 2)
                act.activation(h_hi[:, j:j + 2, :], h_sum[:, j:j + 2, 0:2 * H], ACT.Copy)\
                   .then_inc(h_high, 1)

            def ctx_out(b, q):
                act.wait_ge(ctx_done, 4 * b + q + 1)
                wait(act, back_ready, 2 * b + q // 2)
                c = (q % 2) * QUART
                act.activation(ctxT[:, c:c + QUART], ps_ctx[:, q % 2, :], ACT.Copy)\
                   .then_inc(ctxT_ready, 1)

            def y_out(b, half):
                act.wait_ge(y_done, 2 * b + half + 1)
                act.activation(yT[:, half, :], y_bank(b, half), ACT.Copy).then_inc(yT_ready, 1)

            def normalize(out_, in_, norm, half):
                for k in range(HB):
                    last = act.activation(out_[:, k, :], in_[:, k, :], ACT.Identity,
                                          bias=shift[norm][:, half, k:k + 1],
                                          scale=row_scales[norm][:, half, k:k + 1])
                return last

            def norm_c(b, half):
                act.wait_ge(c_scale, 2 * b + half + 1)
                c = c_rows[:, half, :, :]
                normalize(c, c, "c", half).then_inc(c_norm, 1)

            def norm_x(b, half):
                act.wait_ge(x_scale, 2 * b + half + 1)
                c = c_rows[:, half, :, :]
                normalize(c, c, "x", half).then_inc(x1_ready, 1)

            def norm_f(b, half):
                act.wait_ge(f_scale, 2 * b + half + 1)
                v = fin[:, half, :, :]
                normalize(v, v, "f", half).then_inc(last_norm, 1)
                act.wait_ge(last_norm, half + 1)
                act.dma_start(batch_rows(out, b, half * HALF, (half + 1) * HALF), v)\
                   .then_inc(last_stored, 16)

            def first_batch(b):
                x_high(b, 0)
                x_high(b, 1)
                weights()
                degree(b, 0)
                degree(b, 1)
                exps(b, 0)
                d_high(b, 0)
                exps(b, 1)
                h_part(b, 0)
                degree(b, 2)
                degree(b, 3)
                exps(b, 2)
                h_part(b, 1)
                d_high(b, 1)
                h_part(b, 2)
                a_out(b, 0, 0)
                h_part(b, 3)
                exps(b, 3)
                a_out(b, 0, 1)
                a_out(b, 1, 0)
                degree(b, 4)
                d_high(b, 2)
                exps(b, 4)
                a_out(b, 1, 1)
                d_high(b, 3)
                exps(b, 5)
                degree(b, 5)
                ctx_out(b, 0)
                a_out(b, 2, 0)
                degree(b, 6)
                d_high(b, 4)
                exps(b, 6)
                ctx_out(b, 1)
                a_out(b, 2, 1)
                d_high(b, 5)
                norm_c(b, 0)
                d_high(b, 6)
                exps(b, 7)
                a_out(b, 3, 0)
                a_out(b, 3, 1)
                a_out(b, 4, 0)
                degree(b, 7)
                a_out(b, 4, 1)

            def batch(b, p):
                x_high(b, 0)
                x_high(b, 1)
                a_out(p, 5, 0)
                d_high(p, 7)
                a_out(p, 5, 1)
                a_out(p, 6, 0)
                exps(b, 0)
                a_out(p, 6, 1)
                a_out(p, 7, 0)
                a_out(p, 7, 1)
                ctx_out(p, 2)
                d_high(b, 0)
                exps(b, 1)
                norm_x(p, 0)
                ctx_out(p, 3)
                exps(b, 2)
                h_part(b, 0)
                degree(b, 0)
                d_high(b, 1)
                h_part(b, 1)
                degree(b, 1)
                exps(b, 3)
                norm_c(p, 1)
                h_part(b, 2)
                degree(b, 2)
                exps(b, 4)
                h_part(b, 3)
                d_high(b, 2)
                norm_x(p, 1)
                d_high(b, 3)
                exps(b, 5)
                degree(b, 3)
                ctx_out(b, 0)
                y_out(p, 0)
                degree(b, 4)
                degree(b, 5)
                exps(b, 6)
                degree(b, 6)
                d_high(b, 4)
                ctx_out(b, 1)
                degree(b, 7)
                exps(b, 7)
                d_high(b, 5)
                norm_c(b, 0)
                y_out(p, 1)
                a_out(b, 0, 0)
                d_high(b, 6)
                a_out(b, 0, 1)
                a_out(b, 1, 0)
                a_out(b, 1, 1)
                a_out(b, 2, 0)
                a_out(b, 2, 1)
                a_out(b, 3, 0)
                a_out(b, 3, 1)
                a_out(b, 4, 0)
                a_out(b, 4, 1)

            def last_batch(p):
                a_out(p, 5, 0)
                d_high(p, 7)
                a_out(p, 5, 1)
                a_out(p, 6, 0)
                ctx_out(p, 2)
                a_out(p, 6, 1)
                ctx_out(p, 3)
                a_out(p, 7, 0)
                a_out(p, 7, 1)
                norm_x(p, 0)
                norm_c(p, 1)
                norm_x(p, 1)
                y_out(p, 0)
                y_out(p, 1)
                norm_f(p, 0)
                norm_f(p, 1)

            first_batch(0)
            with act.Fori(1, B) as b:
                batch(b, b - 1)
            last_batch(B - 1)
            for half in range(2):
                act.wait_ge(fin_free[half], 16 * B)
            act.wait_ge(last_stored, 32)

        @block.vector
        def _(dve):
            def f(t):
                return t.bitcast(F32)

            dve.wait_ge(const_gp, 6)

            def weights():
                dve.wait_ge(const_hi, 1)
                dve.tensor_tensor(wT_lo[:, :], ps_m[:, 0, 0:3 * H], f(wT_hi[:, :]), ALU.subtract)\
                   .then_inc(const_ok, 1)
                dve.wait_ge(bias_in, 48)

            def x_low(b, k):
                dve.wait_ge(xt_hi, 2 * b + k + 1)
                c = slice(k * HALF, (k + 1) * HALF)
                dve.tensor_tensor(xT_lo[:, c], turn_bank(X_TURN + k), f(xT_hi[:, c]), ALU.subtract)\
                   .then_inc(xt_split, 1)

            def row_max(b, i):
                g = NB * b + i
                s = slice(i % 2, i % 2 + 1)
                dve.wait_ge(u_ready, g + 1)
                dve.tensor_reduce(nmax[:, s], ps_u[:, :], AX.X, ALU.max, negate=True).then_inc(nmax_ready, 1)
                dve.wait_ge(nmax_ready, g + 1)
                dve.tensor_scalar(nbias[:, s], nmax[:, s], SCALE, None, ALU.mult).then_inc(nbias_ready, 1)

            def masked(b, i):
                g = NB * b + i
                dve.wait_ge(exp_done, g + 1)
                dve.wait_ge(a_in[i], 16 * (b + 1))
                wait(dve, dt_tr, g - 1)
                wait(dve, diag_done, g - 1)
                dve.tensor_tensor_reduce(out=d_rows[:, i % 2, :], in0=e_rows[:, i % 2, :],
                                         in1=a_rows[:, i, :], scale=1.0, scalar=0.0, op0=ALU.mult,
                                         op1=ALU.add, accum_out=dsum[:, i:i + 1]).then_inc(d_ready, 1)

            def finish_d(b, i):
                g, q, c = NB * b + i, i // 2, (i % 2) * P
                dve.wait_ge(d_ready, g + 1)
                wait(dve, diag_done, g)
                wait(dve, self_done, 2 * b + i // HB - 1)
                dve.tensor_tensor_reduce(out=junk[:, :], in0=d_rows[:, i % 2, i * P:(i + 1) * P],
                                         in1=ident[:, :], scale=1.0, scalar=0.0, op0=ALU.mult,
                                         op1=ALU.add, accum_out=ddiag[:, i:i + 1]).then_inc(diag_done, 1)
                dve.wait_ge(dt_hi, g + 1)
                dve.tensor_tensor(dT_lo[:, q % 2, :, c:c + P],
                                  ps_d[:, :, :].rearrange("p k (j c) -> p (k j) c", c=P),
                                  f(dT_hi[:, q % 2, :, c:c + P]), ALU.subtract).then_inc(dt_split, 1)

            def add_bias(b, j):
                if j == 0:
                    wait(dve, self_done, 2 * b)
                dve.wait_ge(h_ready, NB * b + j + 1)
                dve.tensor_tensor(h_sum[:, j, :], h_bank(j)[:, 0:3 * H], bias_bc[:, :], ALU.add)\
                   .then_inc(h_added, 1)

            def add_self(b, half):
                n = 2 * b + half
                dve.wait_ge(back_ready, n + 1)
                dve.wait_ge(self_done, n + 1)
                c = c_rows[:, half, :, :]
                dve.tensor_tensor(c, ps_ctx[:, :, :].rearrange("p a (k h) -> p (a k) h", h=H), c, ALU.add)\
                   .then_inc(back_read, 1)

            def stats_c(b, half):
                n = 2 * b + half
                cols = slice(HB * half, HB * (half + 1))
                base = 3 * n
                dve.scalar_tensor_tensor(out=rn2[:, half, :], in0=zsum[:, cols], scalar=EPS_RENORM,
                                         in1=dsum[:, cols], op0=ALU.mult, op1=ALU.add).then_inc(c_step, 1)
                dve.wait_ge(back_read, n + 1)
                for k in range(HB):
                    last = dve.bn_stats(stats["c"][:, half, k, :], c_rows[:, half, k, :])
                last.then_inc(c_step, 1)
                dve.wait_ge(c_step, base + 2)
                dve.reciprocal(rn[:, half, :], rn2[:, half, :]).then_inc(c_step, 1)
                for k in range(HB):
                    last = dve.bn_aggr(mv["c"][:, half, k, :], stats["c"][:, half, k, :])
                last.then_inc(c_small, 1)
                dve.wait_ge(c_step, base + 3)
                dve.tensor_tensor(rn2[:, half, :], rn[:, half, :], rn[:, half, :], ALU.mult)\
                   .then_inc(c_small, 1)
                dve.wait_ge(c_small, 3 * n + 2)
                dve.tensor_tensor(var["c"][:, half, :], mv["c"][:, half, :, 1], rn2[:, half, :], ALU.mult)\
                   .then_inc(c_small, 1)
                dve.tensor_scalar(nmean["c"][:, half, :], mv["c"][:, half, :, 0], -1.0, None, ALU.mult)\
                   .then_inc(c_var, 1)
                dve.wait_ge(c_small, 3 * n + 3)
                dve.tensor_scalar(var["c"][:, half, :], var["c"][:, half, :], EPS_CTX, None, ALU.add)\
                   .then_inc(c_var, 1)

            def stats_x(b, half):
                n = 2 * b + half
                cols = slice(HB * half, HB * (half + 1))
                base = 3 * n
                dve.wait_ge(affine_b, n + 1)
                dve.wait_ge(xres_in, 16 * (b + 1))
                c = c_rows[:, half, :, :]
                dve.scalar_tensor_tensor(out=c, in0=c, scalar=0.0, in1=x_res[:, cols, :],
                                         op0=ALU.max, op1=ALU.add).then_inc(x_step, 1)
                dve.wait_ge(x_step, base + 1)
                for k in range(HB):
                    last = dve.bn_stats(stats["x"][:, half, k, :], c_rows[:, half, k, :])
                last.then_inc(x_step, 1)
                dve.wait_ge(deg_done, NB * b + HB * (half + 1))
                dve.tensor_scalar(vdeg[:, half, :], deg[:, cols], EPS_DEG, None, ALU.add).then_inc(x_var, 1)
                dve.wait_ge(x_step, base + 2)
                dve.sem_inc(x_step, 1)
                for k in range(HB):
                    last = dve.bn_aggr(mv["x"][:, half, k, :], stats["x"][:, half, k, :])
                last.then_inc(x_small, 1)
                dve.wait_ge(x_small, n + 1)
                dve.tensor_scalar(var["x"][:, half, :], mv["x"][:, half, :, 1], EPS_LN, None, ALU.add)\
                   .then_inc(x_var, 1)
                dve.tensor_scalar(nmean["x"][:, half, :], mv["x"][:, half, :, 0], -1.0, None, ALU.mult)\
                   .then_inc(x_var, 1)

            def add_out(b, half):
                n = 2 * b + half
                dve.wait_ge(o_ready, n + 1)
                dve.wait_ge(fin_free[half], 16 * (b + 1))
                dve.wait_ge(x1b_ready, n + 1)
                dve.wait_ge(dinv_ready, n + 1)
                for k in range(HB):
                    i = HB * half + k
                    last = dve.scalar_tensor_tensor(out=fin[:, half, k, :], in0=o_bank(b, half)[:, k * P:(k + 1) * P],
                                                    scalar=dinv[:, i:i + 1], in1=x1b[:, i, :],
                                                    op0=ALU.mult, op1=ALU.add)
                last.then_inc(o_read, 1)

            def stats_f(b, half):
                n = 2 * b + half
                dve.wait_ge(o_read, n + 1)
                for k in range(HB):
                    last = dve.bn_stats(stats["f"][:, half, k, :], fin[:, half, k, :])
                last.then_inc(f_step, 1)
                dve.wait_ge(f_step, 2 * n + 1)
                dve.sem_inc(f_step, 1)
                for k in range(HB):
                    last = dve.bn_aggr(mv["f"][:, half, k, :], stats["f"][:, half, k, :])
                last.then_inc(f_small, 1)
                dve.wait_ge(f_small, n + 1)
                dve.tensor_scalar(var["f"][:, half, :], mv["f"][:, half, :, 1], EPS_LN, None, ALU.add)\
                   .then_inc(f_var, 1)
                dve.tensor_scalar(nmean["f"][:, half, :], mv["f"][:, half, :, 0], -1.0, None, ALU.mult)\
                   .then_inc(f_var, 1)

            def affine(b, half):
                dve.wait_ge(bcast_in, 48)
                affine_on(dve, b, half)

            def first_batch(b):
                x_low(b, 0)
                x_low(b, 1)
                weights()
                row_max(b, 0)
                add_bias(b, 0)
                add_bias(b, 1)
                masked(b, 0)
                add_bias(b, 2)
                row_max(b, 1)
                add_bias(b, 3)
                finish_d(b, 0)
                masked(b, 1)
                row_max(b, 2)
                add_bias(b, 4)
                add_bias(b, 5)
                add_bias(b, 6)
                add_bias(b, 7)
                row_max(b, 3)
                finish_d(b, 1)
                masked(b, 2)
                row_max(b, 4)
                masked(b, 3)
                finish_d(b, 2)
                masked(b, 4)
                row_max(b, 5)
                finish_d(b, 3)
                masked(b, 5)
                row_max(b, 6)
                finish_d(b, 4)
                masked(b, 6)
                add_self(b, 0)
                stats_c(b, 0)
                finish_d(b, 5)
                row_max(b, 7)
                finish_d(b, 6)
                masked(b, 7)

            def batch(b, p):
                stats_x(p, 0)
                x_low(b, 0)
                x_low(b, 1)
                row_max(b, 0)
                finish_d(p, 7)
                masked(b, 0)
                row_max(b, 1)
                add_bias(b, 0)
                finish_d(b, 0)
                masked(b, 1)
                row_max(b, 2)
                add_bias(b, 1)
                add_bias(b, 2)
                add_self(p, 1)
                add_bias(b, 3)
                stats_c(p, 1)
                row_max(b, 3)
                finish_d(b, 1)
                masked(b, 2)
                add_bias(b, 4)
                add_bias(b, 5)
                row_max(b, 4)
                add_bias(b, 6)
                add_bias(b, 7)
                stats_x(p, 1)
                masked(b, 3)
                finish_d(b, 2)
                row_max(b, 5)
                masked(b, 4)
                finish_d(b, 3)
                masked(b, 5)
                row_max(b, 6)
                add_out(p, 0)
                stats_f(p, 0)
                finish_d(b, 4)
                add_self(b, 0)
                row_max(b, 7)
                stats_c(b, 0)
                finish_d(b, 5)
                masked(b, 6)
                masked(b, 7)
                add_out(p, 1)
                finish_d(b, 6)
                stats_f(p, 1)

            def last_batch(p):
                finish_d(p, 7)
                stats_x(p, 0)
                add_self(p, 1)
                stats_c(p, 1)
                affine(p, 1)
                stats_x(p, 1)
                add_out(p, 0)
                stats_f(p, 0)
                add_out(p, 1)
                stats_f(p, 1)

            first_batch(0)
            with dve.Fori(1, B) as b:
                batch(b, b - 1)
            last_batch(B - 1)

        @block.gpsimd
        def _(pool):
            pool.memset(ident[:, :], 0.0).then_inc(const_gp, 1)
            pool.memset(sides[:, :], 1.0).then_inc(const_gp, 1)
            pool.memset(minus_half[:, :], -0.5).then_inc(const_gp, 1)
            pool.wait_ge(const_gp, 3)
            pool.affine_select(out=ident[:, :], in_=ident[:, :], compare_op=ALU.not_equal, fill=1.0,
                               base=0, pattern=[[-1, P]], channel_multiplier=1).then_inc(const_gp, 1)
            for k, sign in ((0, 1), (1, -1)):
                v = sides[:, k * P:(k + 1) * P]
                pool.affine_select(out=v, in_=v, compare_op=ALU.is_gt, fill=0.0, base=0,
                                   pattern=[[-sign, P]], channel_multiplier=sign).then_inc(const_gp, 1)
            for half in range(2):
                rows = slice(half * (H // 2), (half + 1) * (H // 2))
                pool.dma_start(w1_sb[rows, :], W1[rows, :]).then_inc(fin_free[half], 16)
            pool.wait_ge(const_gp, 6)
            pool.wait_ge(bcast_in, 48)

            def per_row(t):
                return t.rearrange("p (j a) -> p j a", a=1).to_broadcast([P, HB, H])

            def masks(b, i):
                g, slot, ii = NB * b + i, (i // 2) % 2, i % 2
                pool.wait_ge(dt_split, g + 1)
                here, copy = slice(ii * P, (ii + 1) * P), slice(QUART, QUART + P)
                left, right = sides[:, 0:P], sides[:, P:2 * P]
                in_place, in_copy = (right, left) if ii == 0 else (left, right)
                for t in (dT_hi, dT_lo):
                    v, w = t[:, slot, i, here], t[:, slot, i, copy]
                    pool.tensor_tensor(w, v.bitcast(F32), in_copy, ALU.mult).then_inc(mask_done, 1)
                    pool.tensor_tensor(v, v.bitcast(F32), in_place, ALU.mult).then_inc(mask_done, 1)

            def h_low(b, jj):
                j = 2 * jj
                pool.wait_ge(h_high, HB * b + jj + 1)
                pool.tensor_tensor(h_lo[:, j:j + 2, :], h_sum[:, j:j + 2, 0:2 * H],
                                   h_hi[:, j:j + 2, :].bitcast(F32), ALU.subtract).then_inc(h_split, 1)

            def self_term(b, half):
                i = HB * half
                pool.wait_ge(diag_done, NB * b + HB * (half + 1))
                pool.wait_ge(h_added, NB * (b + 1))
                wait(pool, x1b_ready, 2 * b + half - 1)
                pool.tensor_tensor(c_rows[:, half, :, :], h_sum[:, i:i + HB, 2 * H:3 * H],
                                   per_row(ddiag[:, i:i + HB]), ALU.mult).then_inc(self_done, 1)

            def row_scale(norm, half, power_done, scaled, done, n, more=None):
                pool.tensor_tensor(power[norm][:, half, :], var[norm][:, half, :], minus_half[:, :], ALU.pow)\
                    .then_inc(power_done, 1)
                pool.wait_ge(power_done, n + 1)
                s = power[norm]
                if more is not None:
                    s = scale[norm]
                    pool.tensor_tensor(s[:, half, :], power[norm][:, half, :], more[:, half, :], ALU.mult)\
                        .then_inc(scaled, 1)
                    pool.wait_ge(scaled, n + 1)
                pool.tensor_tensor(shift[norm][:, half, :], s[:, half, :], nmean[norm][:, half, :], ALU.mult)\
                    .then_inc(done, 1)

            def scale_c(b, half):
                n = 2 * b + half
                pool.wait_ge(c_var, 2 * (n + 1))
                row_scale("c", half, c_power, c_scaled, c_scale, n, rn)

            def affine(b, half):
                affine_on(pool, b, half)

            def scale_x(b, half):
                n = 2 * b + half
                pool.wait_ge(x_var, 3 * (n + 1))
                row_scale("x", half, x_power, None, x_scale, n)
                i = HB * half
                pool.tensor_tensor(dinv[:, i:i + HB], vdeg[:, half, :], minus_half[:, :], ALU.pow)\
                    .then_inc(dinv_ready, 1)

            def times_degree(b, half):
                n = 2 * b + half
                cols = slice(HB * half, HB * (half + 1))
                pool.wait_ge(x1_ready, n + 1)
                pool.wait_ge(dinv_ready, n + 1)
                pool.tensor_tensor(x1p[:, cols, :], c_rows[:, half, :, :], per_row(dinv[:, cols]), ALU.mult)\
                    .then_inc(x1p_ready, 1)
                pool.tensor_tensor(x1b[:, cols, :], c_rows[:, half, :, :], bc(b1_bc), ALU.add)\
                    .then_inc(x1b_ready, 1)

            def scale_f(b, half):
                n = 2 * b + half
                pool.wait_ge(f_var, 2 * (n + 1))
                row_scale("f", half, f_power, None, f_scale, n)

            def norm_f(b, half):
                n = 2 * b + half
                pool.wait_ge(f_scale, n + 1)
                pool.sem_inc(f_norm, 1)
                for k in range(HB):
                    v = fin[:, half, k, :]
                    last = pool.tensor_scalar(v, v, power["f"][:, half, k:k + 1], shift["f"][:, half, k:k + 1],
                                              ALU.mult, ALU.add)
                last.then_inc(f_norm, 1)
                pool.wait_ge(f_norm, 2 * (n + 1))
                pool.dma_start(batch_rows(out, b, half * HALF, (half + 1) * HALF), fin[:, half, :, :])\
                    .then_inc(fin_free[half], 16)

            def first_batch(b):
                masks(b, 0)
                h_low(b, 0)
                h_low(b, 1)
                h_low(b, 2)
                h_low(b, 3)
                masks(b, 1)
                masks(b, 2)
                masks(b, 3)
                self_term(b, 0)
                masks(b, 4)
                scale_c(b, 0)
                masks(b, 5)
                affine(b, 0)
                masks(b, 6)

            def batch(b, p):
                scale_x(p, 0)
                masks(p, 7)
                self_term(p, 1)
                masks(b, 0)
                times_degree(p, 0)
                h_low(b, 0)
                scale_c(p, 1)
                h_low(b, 1)
                masks(b, 1)
                affine(p, 1)
                h_low(b, 2)
                h_low(b, 3)
                scale_x(p, 1)
                times_degree(p, 1)
                masks(b, 2)
                masks(b, 3)
                self_term(b, 0)
                masks(b, 4)
                scale_c(b, 0)
                masks(b, 5)
                affine(b, 0)
                scale_f(p, 0)
                norm_f(p, 0)
                scale_f(p, 1)
                norm_f(p, 1)
                masks(b, 6)

            def last_batch(p):
                masks(p, 7)
                scale_x(p, 0)
                self_term(p, 1)
                scale_c(p, 1)
                times_degree(p, 0)
                scale_x(p, 1)
                times_degree(p, 1)
                scale_f(p, 0)
                scale_f(p, 1)

            first_batch(0)
            with pool.Fori(1, B) as b:
                batch(b, b - 1)
            last_batch(B - 1)


_INS = ['x', 'adj', 'L0_gnn_Wl', 'L0_gnn_bl', 'L0_gnn_Ws', 'L0_gnn_bs', 'L0_gnn_Wr', 'L0_gnn_br',
        'L0_gnn_ln_w', 'L0_gnn_ln_b', 'L1_gnn_weight', 'L1_gnn_bias']


def kernel(**inputs):
    import numpy as _np
    import concourse.bacc as _bacc
    from concourse import mybir as _mybir
    from concourse.bass_utils import run_bass_kernel_spmd as _run

    nc = _bacc.Bacc("TRN2", target_bir_lowering=False, num_devices=1)
    arrays, args = {}, []
    for name in _INS:
        a = _np.ascontiguousarray(inputs[name])
        arrays[f"in_{name}_dram"] = a
        args.append(nc.dram_tensor(f"in_{name}_dram", a.shape, _mybir.dt.from_np(a.dtype), kind="ExternalInput").ap())
    shape = arrays["in_x_dram"].shape
    args.append(nc.dram_tensor("out_0_dram", shape, _mybir.dt.float32, kind="ExternalOutput").ap())
    two_layer_graph_kernel(nc, *args)
    r = _run(nc, [arrays], core_ids=[0])
    return r.results[0]["out_0_dram"]
```
